# Optimizing a Trainium2 kernel written in Bass

```python
import numpy as np
import jax
import jax.numpy as jnp

def _softmax(x, axis=-1):
    return jax.nn.softmax(x, axis=axis)

def _gelu(x):
    return jax.nn.gelu(x, approximate=True)

def _silu(x):
    return jax.nn.silu(x)

def _sigmoid(x):
    return jax.nn.sigmoid(x)

def _layernorm(x, axis=-1, eps=1e-05):
    m = jnp.mean(x, axis=axis, keepdims=True)
    v = jnp.var(x, axis=axis, keepdims=True)
    return (x - m) / jnp.sqrt(v + eps)

def _scatter_add(tgt, idx, src, axis=0):
    return tgt.at[idx].add(src)

def _segment_sum(src, seg, n):
    return jax.ops.segment_sum(src, seg, n)
kernel_name = 'mk_macaron_d2_jaxref_r8_f95d7f'

def setup_inputs(seed: int=0):
    np.random.seed(seed)
    _w = jnp.asarray

    def _L0_attn_setup():
        import jax, jax.numpy as jnp
        import numpy as np
        B, T, D, H, R = (4, 512, 128, 16, 32)
        DH = D // H
        key = jax.random.key(seed)
        ks = jax.random.split(key, 5)
        s = 0.02
        return {'x': jax.random.normal(ks[0], (B, T, D), dtype=jnp.float32), 'Wq': jax.random.normal(ks[1], (D, D), dtype=jnp.float32) * s, 'bq': jnp.zeros((D,), dtype=jnp.float32), 'Wd': jax.random.normal(ks[2], (D, R), dtype=jnp.float32) * s, 'bd': jnp.zeros((R,), dtype=jnp.float32), 'Wu': jax.random.normal(ks[3], (R, 2 * D), dtype=jnp.float32) * s, 'bu': jnp.zeros((2 * D,), dtype=jnp.float32), 'Wo': jax.random.normal(ks[4], (D, D), dtype=jnp.float32) * s, 'bo': jnp.zeros((D,), dtype=jnp.float32)}
    _L0_attn_in = _L0_attn_setup()

    def _L0_ffn_setup():
        import jax, jax.numpy as jnp
        import numpy as np
        D_MODEL = 128
        key = jax.random.key(seed)
        k_x, k_w, k_a1, k_a2 = jax.random.split(key, 4)
        x = jax.random.normal(k_x, (4, 256, D_MODEL), dtype=jnp.float32)
        weight = jax.random.normal(k_w, (D_MODEL, D_MODEL), dtype=jnp.float32) * 0.02
        aux_weight1 = jax.random.normal(k_a1, (D_MODEL, D_MODEL), dtype=jnp.float32) * 0.02
        aux_weight2 = jax.random.normal(k_a2, (D_MODEL, D_MODEL), dtype=jnp.float32) * 0.02
        bias = jnp.zeros((D_MODEL,), dtype=jnp.float32)
        return {'x': x, 'weight': weight, 'aux_weight1': aux_weight1, 'aux_weight2': aux_weight2, 'bias': bias}
    _L0_ffn_in = _L0_ffn_setup()

    def _L1_attn_setup():
        import math
        import jax, jax.numpy as jnp
        import numpy as np
        B, C, D = (4, 256, 128)
        DQ = DV = 64
        H = 16
        key = jax.random.key(seed)
        kx, kq, kk, kv, kw = jax.random.split(key, 5)
        x = jax.random.normal(kx, (B, C, D), dtype=jnp.float32)
        Q = jax.random.normal(kq, (DQ, D, H), dtype=jnp.float32) / math.sqrt(D)
        K = jax.random.normal(kk, (DQ, D, H), dtype=jnp.float32) / math.sqrt(D)
        V = jax.random.normal(kv, (DV, D, H), dtype=jnp.float32) / math.sqrt(D)
        W = jax.random.normal(kw, (D, DV, H), dtype=jnp.float32) / math.sqrt(DV)
        return {'x': x, 'Q': Q, 'K': K, 'V': V, 'W': W}
    _L1_attn_in = _L1_attn_setup()

    def _L1_ffn_setup():
        import jax, jax.numpy as jnp
        import numpy as np
        B, N, D = (4, 256, 128)
        SPARSITY = 0.01
        key = jax.random.key(seed)
        k1, k2, k3 = jax.random.split(key, 3)
        x = jax.random.normal(k1, (B, N, D), dtype=jnp.float32)
        spatial = jax.random.normal(k2, (D, D), dtype=jnp.float32) * 0.02
        freq = jnp.fft.fft(spatial, axis=-1)
        k = int(D * SPARSITY)
        mag = jnp.abs(freq)
        kth = jax.lax.top_k(mag, k)[0][:, -1:]
        w_sparse = jnp.where(mag >= kth, freq, 0.0 + 0j)
        bias = jax.random.normal(k3, (D,), dtype=jnp.float32) * 0.01
        return {'x': x, 'w_freq_real': jnp.real(w_sparse).astype(jnp.float32), 'w_freq_imag': jnp.imag(w_sparse).astype(jnp.float32), 'bias': bias}
    _L1_ffn_in = _L1_ffn_setup()
    _d = {'L0_attn_x': _L0_attn_in['x'], 'L0_attn_Wq': _L0_attn_in['Wq'], 'L0_attn_bq': _L0_attn_in['bq'], 'L0_attn_Wd': _L0_attn_in['Wd'], 'L0_attn_bd': _L0_attn_in['bd'], 'L0_attn_Wu': _L0_attn_in['Wu'], 'L0_attn_bu': _L0_attn_in['bu'], 'L0_attn_Wo': _L0_attn_in['Wo'], 'L0_attn_bo': _L0_attn_in['bo'], 'L0_ffn_weight': _L0_ffn_in['weight'], 'L0_ffn_aux_weight1': _L0_ffn_in['aux_weight1'], 'L0_ffn_aux_weight2': _L0_ffn_in['aux_weight2'], 'L0_ffn_bias': _L0_ffn_in['bias'], 'L1_attn_Q': _L1_attn_in['Q'], 'L1_attn_K': _L1_attn_in['K'], 'L1_attn_V': _L1_attn_in['V'], 'L1_attn_W': _L1_attn_in['W'], 'L1_ffn_w_freq_real': _L1_ffn_in['w_freq_real'], 'L1_ffn_w_freq_imag': _L1_ffn_in['w_freq_imag'], 'L1_ffn_bias': _L1_ffn_in['bias']}
    _x0 = _d['L0_attn_x']
    _d['L0_attn_x'] = jax.random.normal(jax.random.fold_in(jax.random.key(seed), 1), (32, 256, 128), dtype=_x0.dtype)
    del _x0
    return _d

def reference(L0_attn_x, L0_attn_Wq, L0_attn_bq, L0_attn_Wd, L0_attn_bd, L0_attn_Wu, L0_attn_bu, L0_attn_Wo, L0_attn_bo, L0_ffn_weight, L0_ffn_aux_weight1, L0_ffn_aux_weight2, L0_ffn_bias, L1_attn_Q, L1_attn_K, L1_attn_V, L1_attn_W, L1_ffn_w_freq_real, L1_ffn_w_freq_imag, L1_ffn_bias):

    def _L0_attn_ref(x, Wq, bq, Wd, bd, Wu, bu, Wo, bo):
        import jax, jax.numpy as jnp
        import numpy as np
        B, T, D, H, R = (4, 512, 128, 16, 32)
        DH = D // H
        b, t = (x.shape[0], x.shape[1])
        q = (x @ Wq + bq).reshape(b, t, H, DH)
        kv = ((x @ Wd + bd) @ Wu + bu).reshape(b, t, H, 2 * DH)
        k, v = (kv[..., :DH], kv[..., DH:])
        q = jax.nn.elu(q) + 1.0
        k = jax.nn.elu(k) + 1.0
        context = jnp.einsum('bthd,bthe->bhde', k, v)
        out = jnp.einsum('bthd,bhde->bthe', q, context)
        k_sum = k.sum(axis=1)
        z = 1.0 / (jnp.einsum('bthd,bhd->bth', q, k_sum) + 1e-06)
        out = out * z[..., None]
        return out.reshape(b, t, D) @ Wo + bo

    def _L0_ffn_ref(x, weight, aux_weight1, aux_weight2, bias):
        import jax, jax.numpy as jnp
        import numpy as np
        D_MODEL = 128
        h = jnp.einsum('btc,cd->btd', x, weight)
        h = jnp.einsum('btc,cd->btd', h, aux_weight1)
        h = jnp.einsum('btc,cd->btd', h, aux_weight2)
        return jnp.tanh(h + bias)

    def _L1_attn_ref(x, Q, K, V, W):
        import math
        import jax, jax.numpy as jnp
        import numpy as np
        B, C, D = (4, 256, 128)
        DQ = DV = 64
        H = 16
        d_query, d_embed, num_heads = Q.shape
        d_value = V.shape[0]
        sq = math.sqrt(d_query / d_embed)
        sv = math.sqrt(d_value / d_embed)
        q = jnp.einsum('qdh,bcd->bhcq', Q, x) * sq
        k = jnp.einsum('qdh,bcd->bhcq', K, x) * sq
        v = jnp.einsum('vdh,bcd->bhcv', V, x) * sv
        att = jnp.einsum('bhcq,bhCq->bhcC', q, k) / d_query
        T = x.shape[1]
        causal = jnp.arange(T)[:, None] >= jnp.arange(T)[None, :]
        att = jnp.where(causal, att, -jnp.inf)
        p = jax.nn.softmax(att, axis=-1)
        y = jnp.einsum('bhcC,bhCv->bhcv', p, v)
        z = jnp.einsum('dvh,bhcv->bcd', W, y) * (math.sqrt(d_embed / d_value) / num_heads)
        return z

    def _L1_ffn_ref(x, w_freq_real, w_freq_imag, bias):
        import jax, jax.numpy as jnp
        import numpy as np
        B, N, D = (4, 256, 128)
        SPARSITY = 0.01
        w = jax.lax.complex(w_freq_real, w_freq_imag)
        x_freq = jnp.fft.fft(x, axis=-1)
        y_freq = jnp.einsum('bnd,do->bno', x_freq, w)
        y = jnp.real(jnp.fft.ifft(y_freq, axis=-1))
        return y + bias
    x = L0_attn_x
    x = x + 0.5 * _L0_ffn_ref(_layernorm(x, axis=-1), L0_ffn_weight, L0_ffn_aux_weight1, L0_ffn_aux_weight2, L0_ffn_bias)
    x = x + _L0_attn_ref(_layernorm(x, axis=-1), L0_attn_Wq, L0_attn_bq, L0_attn_Wd, L0_attn_bd, L0_attn_Wu, L0_attn_bu, L0_attn_Wo, L0_attn_bo)
    x = x + 0.5 * _L0_ffn_ref(_layernorm(x, axis=-1), L0_ffn_weight, L0_ffn_aux_weight1, L0_ffn_aux_weight2, L0_ffn_bias)
    x = x + 0.5 * _L1_ffn_ref(_layernorm(x, axis=-1), L1_ffn_w_freq_real, L1_ffn_w_freq_imag, L1_ffn_bias)
    x = x + _L1_attn_ref(_layernorm(x, axis=-1), L1_attn_Q, L1_attn_K, L1_attn_V, L1_attn_W)
    x = x + 0.5 * _L1_ffn_ref(_layernorm(x, axis=-1), L1_ffn_w_freq_real, L1_ffn_w_freq_imag, L1_ffn_bias)
    return x

_drawn_inputs = setup_inputs


def setup_inputs(seed=0):
    import zlib

    import numpy as np

    out = dict(_drawn_inputs(seed))
    spreads = {'L0_attn_bq': (0.0, 2.0),
     'L0_attn_bd': (0.0, 0.8),
     'L0_attn_bu': (0.0, 0.306),
     'L0_attn_bo': (0.0, 0.1),
     'L0_ffn_bias': (0.0, 0.1)}
    factors = {'L0_attn_Wq': 25.951,
     'L0_attn_Wd': 8.0,
     'L0_attn_Wu': 8.0,
     'L0_ffn_weight': 4.997,
     'L0_ffn_aux_weight1': 4.945,
     'L0_ffn_aux_weight2': 5.054,
     'L1_attn_Q': 8.0,
     'L1_attn_K': 8.0,
     'L1_ffn_bias': 6.131}
    for name, (base, spread) in spreads.items():
        noise = np.random.default_rng([zlib.crc32(name.encode()), seed]).standard_normal(out[name].shape)
        drawn = base * np.exp(spread * noise) if base else spread * noise
        out[name] = jnp.asarray(drawn.astype(out[name].dtype))
    for name, factor in factors.items():
        out[name] = (out[name] * factor).astype(out[name].dtype)
    return out
```

```python
import concourse.bass as bass
import numpy as np
from concourse import mybir
from contextlib import ExitStack

F32 = mybir.dt.float32
F32R = mybir.dt.float32r
BF16 = mybir.dt.bfloat16
ALU = mybir.AluOpType
ACT = mybir.ActivationFunctionType
AX = mybir.AxisListType

B, T, D = 32, 256, 128
P = 128
TILES = B * T // P
BT = T // P
G = 16
GT = TILES // G
GB = B // G
GW = GT * D
H0, R = 16, 32
E0 = D // H0
H, DQ, DV = 16, 64, 64
PAIRS = H // 2
EPS = 1e-5
Z_EPS = 1e-6
MASKED = -3.0e38
SCORE_SCALE = 1.0 / D
OUT_SCALE = 1.0 / H
LEAD = 3


class Count:

    def __init__(self, i, step=1, base=0):
        self.i, self.step, self.base = i, step, base

    def __add__(self, n):
        return Count(self.i, self.step, self.base + n)

    __radd__ = __add__

    def __sub__(self, n):
        return self + -n

    def __mul__(self, n):
        return Count(self.i, self.step * n, self.base * n)

    __rmul__ = __mul__


def count(n):
    return n.i * n.step + n.base if isinstance(n, Count) else n


def groups(eng, stages):
    def turn(t):
        for lead, f in stages:
            if 0 <= t + lead < G:
                f(t + lead, (t + lead) % 2)
    for t in range(-LEAD, 2):
        turn(t)
    last = (G - LEAD) // 2
    with eng.Fori(1, last) as i:
        for j in range(2):
            for lead, f in stages:
                f(Count(i, 2, j + lead), (j + lead) % 2)
    for t in range(2 * last, G):
        turn(t)


def batches(eng, batch):
    batch(0, 0, first=True)
    batch(1, 1)
    with eng.Fori(1, B // 2 - 1) as i:
        for j in range(2):
            batch(Count(i, 2, j), j)
    batch(B - 2, 0)
    batch(B - 1, 1, last=True)


def above_0(n):
    return isinstance(n, Count) or n > 0


def build(nc, x, Wq, bq, Wd, bd, Wu, bu, Wo, bo, W1, W2, W3, ffn_bias, Q, K, V, W, w_re, w_im, fft_bias, dft, out):
    ctx = ExitStack()
    with ctx:
        def sb(name, shape, dt=F32):
            return ctx.enter_context(nc.sbuf_tensor(name, shape, dt))

        def sem(name):
            return ctx.enter_context(nc.semaphore(name))

        x_all = sb("x_all", [P, TILES * D])
        ident = sb("ident", [P, P])
        ident_bf = sb("ident_bf", [P, P], BF16)
        mask_bf = sb("mask_bf", [P, 2, P], BF16)
        ones_bf = sb("ones_bf", [P, 512], BF16)
        head_mask = sb("head_mask", [P, 4, P])
        wq_s = sb("wq_s", [P, D]); wd_s = sb("wd_s", [P, R]); wu_s = sb("wu_s", [R, 2 * D])
        bd_s = sb("bd_s", [R, 1]); wo_s = sb("wo_s", [P, D])
        w123_s = sb("w123_s", [P, 3, D]); wre_s = sb("wre_s", [P, D]); wim_s = sb("wim_s", [P, D])
        dft_s = sb("dft_s", [P, 3, D])
        rows = sb("rows", [1, 4 * D + 2 * D])
        BQ, BFFN, BFFT, BO, BU = 0, D, 2 * D, 3 * D, 4 * D
        space = sb("space", [P, 2 * BT * H * DV + 2 * PAIRS * T])
        q_raw, k_raw, v_raw = (space[0:DQ, k * D * H:(k + 1) * D * H] for k in range(3))
        w_raw = space[:, 3 * D * H:3 * D * H + DV * H]
        w_heads = space[:, 3 * D * H + DV * H:3 * D * H + 2 * DV * H]
        wt_s = sb("wt_s", [P, 3, D])
        w23 = sb("w23", [P, D]); wc = sb("wc", [P, D])
        wkv = sb("wkv", [P, 2 * D])
        abT = sb("abT", [P, 2, D]); circ = sb("circ", [P, D])
        bias_bf = sb("bias_bf", [P, 4, 512], BF16)
        biasq_bf = sb("biasq_bf", [P, P], BF16)
        FFN_B, FFT_B, BO_B, KV_B = range(4)
        kvrow = sb("kvrow", [1, 2 * D])
        rest = sb("rest", [1, 2, 512])
        bwide = sb("bwide", [1, 5, 512])
        g_hi = sb("g_hi", [P, H, D], F32R); g_lo = sb("g_lo", [P, H, D], F32R)
        v_hi = sb("v_hi", [P, H * DV], F32R); v_lo = sb("v_lo", [P, H * DV], F32R)
        wz = sb("wz", [P, PAIRS, D])
        half_neg = sb("half_neg", [P, GT]); eps_t = sb("eps_t", [P, GT])
        bst = sb("bst", [P, 2, GT, 6]); mv = sb("mv", [P, 2, GT, 2])
        veps = sb("veps", [P, 2, GT]); rstd = sb("rstd", [P, 2, GT])
        pause = sb("pause", [P, 1])
        xn = sb("xn", [P, 2, GW])
        xT = sb("xT", [P, 2, GW])
        th = sb("th", [P, 2, GW])
        eq = sb("eq", [P, GW]); ek = sb("ek", [P, GT, P])
        phq = sb("phq", [P, 2, GW]); phk = sb("phk", [P, GT, P])
        vones = sb("vones", [P, GT, 2 * P])
        cbd = sb("cbd", [P, GB, 2 * P])
        zr = sb("zr", [P, GW]); yT0 = sb("yT0", [P, GW])
        x_hi = sb("x_hi", [P, 2, T], F32R); x_lo = sb("x_lo", [P, 2, T], F32R)
        u_hi = sb("u_hi", [P, 2, 2, T], F32R); u_lo = sb("u_lo", [P, 2, 2, T], F32R)
        nmax = sb("nmax", [P, 2, 4]); rsum = sb("rsum", [P, 2, 4]); rinv = sb("rinv", [P, 2, 4])
        pr = sb("pr", [P, 2, 2, 3, P])
        pT = sb("pT", [P, 2, 2, 3, P])
        vv = space[:, 0:2 * BT * H * DV].rearrange("p (r t n) -> p r t n", r=2, t=BT)
        yT = space[:, 2 * BT * H * DV:].rearrange("p (r a t) -> p r a t", r=2, a=PAIRS)

        ps = ctx.enter_context(nc.psum_tensor("ps", [P, 8, 512], F32))

        in_first = sem("in_first"); in_rest = sem("in_rest")
        in_small = sem("in_small"); in_qk = sem("in_qk"); in_vw = sem("in_vw")
        pool_const = sem("pool_const"); dve_const = sem("dve_const")
        su_pe = sem("su_pe"); su_ev = sem("su_ev"); su_row = sem("su_row"); su_x = sem("su_x")
        su_hi = sem("su_hi"); su_lo = sem("su_lo"); w_heads_ready = sem("w_heads_ready")
        stats_done = sem("stats_done"); mv_ready = sem("mv_ready")
        pool_step = sem("pool_step"); rstd_ready = sem("rstd_ready")
        xn_ready = sem("xn_ready"); tr_done = sem("tr_done"); xT_ready = sem("xT_ready")
        mm_done = sem("mm_done"); th_ready = sem("th_ready"); x_ready = sem("x_ready")
        q_done = sem("q_done"); kv_done = sem("kv_done"); ek_ready = sem("ek_ready"); eq_ready = sem("eq_ready"); v0_ready = sem("v0_ready"); phi_ready = sem("phi_ready")
        ctx_done = sem("ctx_done"); cbd_ready = sem("cbd_ready"); nd_done = sem("nd_done")
        den_ready = sem("den_ready"); zr_ready = sem("zr_ready"); y0_ready = sem("y0_ready")
        u_done = sem("u_done"); uhi_ready = sem("uhi_ready"); ulo_ready = sem("ulo_ready")
        s_done = sem("s_done"); max_ready = sem("max_ready"); exp_ready = sem("exp_ready")
        rinv_ready = sem("rinv_ready"); pn_ready = sem("pn_ready"); pt_done = sem("pt_done")
        pTa_ready = sem("pTa_ready"); pTb_ready = sem("pTb_ready")
        pv_done = sem("pv_done"); y_ready = sem("y_ready")
        v_done = sem("v_done"); v_ready = sem("v_ready"); w_done = sem("w_done")
        xhi_ready = sem("xhi_ready"); xlo_ready = sem("xlo_ready")
        out_done = sem("out_done")

        block = ctx.enter_context(nc.Block())
        SMALL_LOADS = 16

        def xg(g, t=0, n=GT):
            return x_all[:, bass.ds(count(g * GW + t * D), n * D)]

        def xb(b, t=0, n=BT):
            return x_all[:, bass.ds(count(b * (BT * D) + t * D), n * D)]

        LIN_Q, LIN_KV, LIN_C, LIN_N, LIN_D, LIN_O = 1, 2, 4, 5, 6, 7
        kv = ps[:, LIN_KV:LIN_KV + 2, :].rearrange("p b (t n) -> p (b t) n", n=2 * P)
        BANK_OUT = 2
        BANK_U, BANK_S, BANK_X, BANK_T = 0, 1, 5, 6
        y_bank = ps[:, BANK_T + 1, 512 - T:512]

        FFN1, LIN, FFN2, SPEC1, SPEC2 = range(5)
        X_BEFORE = {FFN1: 0, LIN: G, FFN2: 2 * G, SPEC1: 3 * G, SPEC2: 4 * G + B}
        X_SOFT = 4 * G
        LN_SOFT = 4 * G

        def ln_no(phase, g):
            return g + (phase * G if phase < SPEC2 else LN_SOFT + B)

        V_TURN = 4

        @block.sync
        def _(sp):
            def tiles_of(a, b0, b1):
                return a[b0:b1].rearrange("b (t p) d -> p (b t) d", p=P)
            sp.dma_start(x_all[:, 0:2 * GW].rearrange("p (t d) -> p t d", d=D), tiles_of(x, 0, 2 * GB)).then_inc(in_first, 16)
            sp.dma_start(x_all[:, 2 * GW:].rearrange("p (t d) -> p t d", d=D), tiles_of(x, 2 * GB, B)).then_inc(in_rest, 16)
            sp.dma_start(q_raw, Q.rearrange("q d h -> q (d h)")).then_inc(in_qk, 16)
            sp.dma_start(k_raw, K.rearrange("q d h -> q (d h)")).then_inc(in_qk, 16)
            sp.dma_start(v_raw, V.rearrange("q d h -> q (d h)")).then_inc(in_vw, 16)
            sp.dma_start(w_raw, W.rearrange("d v h -> d (v h)")).then_inc(in_vw, 16)
            with sp.Fori(0, G) as i:
                g = Count(i)
                sp.wait_ge(x_ready, count(g + (X_BEFORE[SPEC2] + 1)))
                sp.dma_start(out[bass.ds(count(g * GB), GB)].rearrange("b (t p) d -> p (b t) d", p=P),
                             xg(g).rearrange("p (t d) -> p t d", d=D)).then_inc(out_done, 16)
            sp.wait_ge(out_done, 16 * G)

        @block.gpsimd
        def _(pool):
            nc.gpsimd.memset(ident[:], 0.0).then_inc(pool_step, 1)
            nc.gpsimd.memset(mask_bf[:], 0.0).then_inc(pool_step, 1)
            nc.gpsimd.memset(head_mask[:], 1.0).then_inc(pool_step, 1)
            nc.gpsimd.memset(half_neg[:], -0.5)
            nc.gpsimd.memset(eps_t[:], EPS)
            nc.gpsimd.memset(ones_bf[:], 1.0)
            nc.gpsimd.memset(vones[:], 1.0)
            pool.wait_ge(pool_step, 3)
            nc.gpsimd.affine_select(out=ident[:], in_=ident[:], compare_op=ALU.not_equal, fill=1.0, base=0,
                                    pattern=[[-1, P]], channel_multiplier=1).then_inc(pool_const, 1)
            nc.gpsimd.affine_select(out=mask_bf[:], in_=mask_bf[:], compare_op=ALU.is_ge, fill=MASKED, base=0,
                                    pattern=[[0, 2], [-1, P]], channel_multiplier=1).then_inc(pool_const, 1)
            hm = head_mask[:].rearrange("p a (h e) -> p (a h) e", e=E0)
            nc.gpsimd.affine_select(out=hm, in_=hm, compare_op=ALU.is_ge, fill=0.0, base=0,
                                    pattern=[[0, 4], [-E0, H0], [0, E0]], channel_multiplier=1).then_inc(pool_step, 1)
            pool.wait_ge(pool_step, 4)
            nc.gpsimd.affine_select(out=hm, in_=hm, compare_op=ALU.is_ge, fill=0.0, base=E0 - 1,
                                    pattern=[[0, 4], [E0, H0], [0, E0]], channel_multiplier=-1).then_inc(pool_const, 1)
            POOL0 = 4
            pool.wait_ge(in_vw, 32)
            nc.gpsimd.tensor_copy(w_heads.rearrange("d (h v) -> d h v", h=H),
                                  w_raw.rearrange("d (v h) -> d h v", h=H)).then_inc(w_heads_ready, 1)

            def inv_std(n, j, w):
                pool.wait_ge(mv_ready, count(n + 1))
                if above_0(n - 1):
                    pool.wait_ge(xn_ready, count(n - 1))
                nc.gpsimd.tensor_tensor(veps[:, j, 0:w], mv[:, j, 0:w, 1], eps_t[:, 0:w], ALU.add).then_inc(pool_step, 1)
                pool.wait_ge(pool_step, count(n + (POOL0 + 1)))
                nc.gpsimd.tensor_tensor(rstd[:, j, 0:w], veps[:, j, 0:w], half_neg[:, 0:w], ALU.pow).then_inc(rstd_ready, 1)

            for phase in (FFN1, LIN, FFN2, SPEC1):
                groups(pool, [(2, lambda g, j: inv_std(ln_no(phase, g), j, GT))])

            def scale_probs(n, j):
                pool.wait_ge(rinv_ready, count(n + 1))
                r = rinv[:, j, :].rearrange("p (h q) -> p h q", h=2)
                nc.gpsimd.tensor_tensor(pr[:, j, :, 0, :], pr[:, j, :, 0, :],
                                        r[:, :, 0:1].to_broadcast([P, 2, P]), ALU.mult)
                nc.gpsimd.tensor_tensor(pr[:, j, :, 1:3, :].rearrange("p h b k -> p h (b k)"),
                                        pr[:, j, :, 1:3, :].rearrange("p h b k -> p h (b k)"),
                                        r[:, :, 1:2].to_broadcast([P, 2, 2 * P]), ALU.mult).then_inc(pn_ready, 1)

            inv_std(LN_SOFT, 0, BT)

            def batch(b, jb, first=False, last=False):
                for p in range(PAIRS):
                    scale_probs(b * PAIRS + p, p % 2)
                    if p == 1 and not last:
                        inv_std(b + (LN_SOFT + 1), 1 - jb, BT)

            batches(pool, batch)
            groups(pool, [(2, lambda g, j: inv_std(ln_no(SPEC2, g), j, GT))])

        @block.vector
        def _(dve):
            nc.vector.memset(bias_bf[:], 0.0)
            nc.vector.memset(biasq_bf[:], 0.0)
            nc.vector.memset(kvrow[:], 0.0).then_inc(dve_const, 1)
            dve.wait_ge(pool_const, 1)
            nc.vector.tensor_copy(ident_bf[:], ident[:]).then_inc(dve_const, 1)
            dve.wait_ge(in_small, 16 * SMALL_LOADS)
            row = [0]

            def rowstep(ins):
                row[0] += 1
                ins.then_inc(su_row, 1)
                dve.wait_ge(su_row, count(row[0]))

            def rep(dst, at, n, times):
                src = rows[0:1, at:at + n].unsqueeze(1).to_broadcast([1, times, n])
                return nc.vector.tensor_copy(dst.rearrange("p (a n) -> p a n", a=times), src)

            rowstep(rep(bwide[:, FFN_B, :], BFFN, D, 4))
            rowstep(rep(bwide[:, FFT_B, :], BFFT, D, 4))
            rowstep(nc.vector.tensor_scalar(bwide[:, FFT_B, :], bwide[:, FFT_B, :], 0.5, None, ALU.mult))
            rowstep(rep(bwide[:, BO_B, :], BO, D, 4))
            dve.wait_ge(su_pe, 3)
            bu_kv = rows[0:1, BU:BU + 2 * D].rearrange("p (h s e) -> p s h e", s=2, e=E0)
            for s in range(2):
                rowstep(nc.vector.tensor_tensor(kvrow[:, s * D:(s + 1) * D].rearrange("p (h e) -> p h e", e=E0),
                                                ps[0:1, 4, s * D:(s + 1) * D].rearrange("p (h e) -> p h e", e=E0),
                                                bu_kv[:, s], ALU.add))
            rowstep(nc.vector.tensor_scalar(kvrow[:, 0:D], kvrow[:, 0:D], 1.0, None, ALU.add))
            rowstep(nc.vector.tensor_copy(bwide[:, KV_B, :].rearrange("p (a n) -> p a n", a=2),
                                          kvrow[:].unsqueeze(1).to_broadcast([1, 2, 2 * D])))
            rowstep(nc.vector.tensor_scalar(bwide[:, 4, 0:D], rows[:, BQ:BQ + D], 1.0, None, ALU.add))
            for i in range(5):
                n = 512 if i < 4 else D
                dst = bias_bf[:, i, :] if i < 4 else biasq_bf[:]
                cur = bwide[:, i, 0:n]
                for part in range(3):
                    piece = dst[32 * part:32 * part + 1, 0:n]
                    rowstep(nc.vector.tensor_copy(piece, cur))
                    if part < 2:
                        nxt = rest[:, part, 0:n]
                        rowstep(nc.vector.tensor_copy(nxt, piece))
                        rowstep(nc.vector.tensor_tensor(nxt, cur, nxt, ALU.subtract))
                        cur = nxt
            nc.vector.memset(kvrow[:, 0:1], 0.0).then_inc(su_x, 1)

            def big_lo():
                for i in range(4):
                    dve.wait_ge(su_hi, count(i + 1))
                    nc.vector.scalar_tensor_tensor(out=g_lo[:, 4 * i:4 * i + 4, :].rearrange("p h d -> p (h d)"),
                                                   in0=ps[:, i % 4, :], scalar=SCORE_SCALE,
                                                   in1=g_hi[:, 4 * i:4 * i + 4, :].rearrange("p h d -> p (h d)").bitcast(F32),
                                                   op0=ALU.mult, op1=ALU.subtract).then_inc(su_lo, 1)
                for i in range(2):
                    dve.wait_ge(su_hi, count(4 + i + 1))
                    nc.vector.tensor_tensor(v_lo[:, 512 * i:512 * i + 512], ps[:, 4 + i, :],
                                            v_hi[:, 512 * i:512 * i + 512].bitcast(F32), ALU.subtract).then_inc(su_lo, 1)
            big_lo()

            def stats(n, xs, w, j, x_at):
                if above_0(x_at):
                    dve.wait_ge(x_ready, count(x_at))
                for t in range(w):
                    last = nc.vector.bn_stats(bst[:, j, t, :], xs(t))
                last.then_inc(stats_done, 1)
                dve.wait_ge(stats_done, count(n + 1))
                nc.vector.memset(pause[:], 0.0)
                for t in range(w):
                    last = nc.vector.bn_aggr(mv[:, j, t, :], bst[:, j, t, :])
                last.then_inc(mv_ready, 1)

            def normalise(n, xs, w, j):
                dve.wait_ge(rstd_ready, count(n + 1))
                if above_0(n - 1):
                    dve.wait_ge(tr_done, count(n - 1))
                for t in range(w):
                    last = nc.vector.tensor_scalar(xn[:, j, t * D:(t + 1) * D], xs(t), mv[:, j, t, 0:1],
                                                   rstd[:, j, t:t + 1], ALU.subtract, ALU.mult)
                last.then_inc(xn_ready, 1)

            def g_stats(phase):
                return lambda g, j: stats(ln_no(phase, g), lambda t: xg(g, t, 1), GT, j,
                                          {FFN1: 0, SPEC2: X_BEFORE[SPEC2]}.get(phase, g + ((phase - 1) * G + 1)))

            def g_norm(phase):
                return lambda g, j: normalise(ln_no(phase, g), lambda t: xg(g, t, 1), GT, j)

            dve.wait_ge(in_first, 16)
            dve.wait_ge(in_rest, 16)

            def add_tanh(k):
                def f(g, j):
                    dve.wait_ge(th_ready, count(g + (k * G + 1)))
                    nc.vector.scalar_tensor_tensor(out=xg(g), in0=th[:, j, :], scalar=0.5, in1=xg(g),
                                                   op0=ALU.mult, op1=ALU.add).then_inc(x_ready, 1)
                return f

            def add_bank(done, base, bank):
                def f(g, j):
                    dve.wait_ge(done, count(g + (base + 1)))
                    nc.vector.tensor_tensor(xg(g), ps[:, bank(j), :], xg(g), ALU.add).then_inc(x_ready, 1)
                return f

            groups(dve, [(3, g_stats(FFN1)), (2, g_norm(FFN1)), (0, add_tanh(0))])

            def phi_k(g, j):
                dve.wait_ge(v0_ready, count(g + 1))
                if above_0(g):
                    dve.wait_ge(ctx_done, count(g))
                nc.vector.scalar_tensor_tensor(out=phk[:], in0=ek[:], scalar=1.0, in1=kv[:, :, 0:P],
                                               op0=ALU.min, op1=ALU.max).then_inc(phi_ready, 1)

            def phi_q(g, j):
                dve.wait_ge(eq_ready, count(g + 1))
                if above_0(g - 1):
                    dve.wait_ge(nd_done, count(g - 1))
                nc.vector.scalar_tensor_tensor(out=phq[:, j, :], in0=eq[:], scalar=1.0, in1=ps[:, LIN_Q, :],
                                               op0=ALU.min, op1=ALU.max).then_inc(phi_ready, 1)

            def context_mask(g, j):
                dve.wait_ge(ctx_done, count(g + 1))
                if above_0(g):
                    dve.wait_ge(nd_done, count(g))
                nc.vector.tensor_tensor(cbd[:].rearrange("p b n -> p (b n)"), ps[:, LIN_C, :],
                                        head_mask[:].rearrange("p a n -> p (a n)"), ALU.mult).then_inc(cbd_ready, 1)

            def z_and_y(g, j):
                dve.wait_ge(den_ready, count(g + 1))
                nc.vector.reciprocal(zr[:], zr[:]).then_inc(zr_ready, 1)
                dve.wait_ge(zr_ready, count(g + 1))
                dve.wait_ge(mm_done, count(g + G))
                nc.vector.tensor_tensor(yT0[:], ps[:, LIN_N, :], zr[:], ALU.mult).then_inc(y0_ready, 1)

            groups(dve, [(2, g_norm(LIN)), (1, phi_k), (1, phi_q), (3, g_stats(LIN)), (0, z_and_y),
                         (1, context_mask), (0, add_bank(mm_done, G, lambda j: LIN_O))])
            groups(dve, [(3, g_stats(FFN2)), (2, g_norm(FFN2)), (0, add_tanh(1))])
            groups(dve, [(3, g_stats(SPEC1)), (2, g_norm(SPEC1)), (0, add_bank(mm_done, 3 * G, lambda j: BANK_OUT + j))])

            def ln_soft_stats(b, j):
                stats(b + LN_SOFT, lambda t: xb(b, t, 1), BT, j, 4 * G)

            def ln_soft_norm(b, j):
                normalise(b + LN_SOFT, lambda t: xb(b, t, 1), BT, j)

            def x_low(b, j):
                dve.wait_ge(xhi_ready, count(b + 1))
                nc.vector.tensor_tensor(x_lo[:, j, :], ps[:, BANK_X, 0:T], x_hi[:, j, :].bitcast(F32), ALU.subtract).then_inc(xlo_ready, 1)

            def u_low(n, j):
                dve.wait_ge(uhi_ready, count(n + 1))
                if above_0(2 * n - 2):
                    dve.wait_ge(s_done, count(2 * n - 2))
                nc.vector.tensor_tensor(u_lo[:, j].rearrange("p h k -> p (h k)"), ps[:, BANK_U, :],
                                        u_hi[:, j].rearrange("p h k -> p (h k)").bitcast(F32), ALU.subtract).then_inc(ulo_ready, 1)

            def neg_max(n, j):
                out4 = nmax[:, j, :].rearrange("p (h q) -> p h q", h=2)
                dve.wait_ge(s_done, count(2 * n + 1))
                if above_0(2 * n - 2):
                    dve.wait_ge(exp_ready, count(2 * n - 2))
                nc.vector.tensor_reduce(out4[:, :, 0], ps[:, BANK_S + 2 * j, 0:2 * P].rearrange("p (h k) -> p h k", h=2),
                                        AX.X, ALU.max, negate=True).then_inc(max_ready, 1)
                dve.wait_ge(s_done, count(2 * n + 2))
                nc.vector.tensor_reduce(out4[:, :, 1], ps[:, BANK_S + 2 * j + 1, :].rearrange("p (h k) -> p h k", h=2),
                                        AX.X, ALU.max, negate=True).then_inc(max_ready, 1)

            def inv_sum(n, j):
                dve.wait_ge(exp_ready, count(2 * n + 2))
                if above_0(n - 1):
                    dve.wait_ge(pn_ready, count(n - 1))
                nc.vector.reciprocal(rinv[:, j, :], rsum[:, j, :]).then_inc(rinv_ready, 1)

            def probs_T(n, j):
                dve.wait_ge(pt_done, count(n + 1))
                if above_0(n - 1):
                    dve.wait_ge(pv_done, count(n - 1))
                nc.vector.tensor_copy(pT[:, j].rearrange("p h b q -> p (h b q)")[:, 0:512],
                                      ps[:, BANK_T, :]).then_inc(pTa_ready, 1)

            def add_z(b, j):
                dve.wait_ge(w_done, count(b + 1))
                nc.vector.tensor_tensor(xb(b), ps[:, BANK_X, 0:BT * D], xb(b), ALU.add).then_inc(x_ready, 1)

            ln_soft_stats(0, 0)
            ln_soft_norm(0, 0)
            x_low(0, 0)
            u_low(0, 0)
            u_low(1, 1)
            neg_max(0, 0)
            u_low(2, 0)
            neg_max(1, 1)

            def batch(b, jb, first=False, last=False):
                for p in range(PAIRS):
                    n, j = b * PAIRS + p, p % 2
                    inv_sum(n, j)
                    if not (first and p == 0):
                        probs_T(n - 1, 1 - j)
                    if not (last and p >= PAIRS - 3):
                        u_low(n + 3, 1 - j)
                    if not (last and p >= PAIRS - 2):
                        neg_max(n + 2, j)
                    if p == 0 and not last:
                        ln_soft_stats(b + 1, 1 - jb)
                    if p == 1 and not first:
                        add_z(b - 1, 1 - jb)
                    if p == 1 and not last:
                        ln_soft_norm(b + 1, 1 - jb)
                    if p == 2 and not last:
                        x_low(b + 1, 1 - jb)

            batches(dve, batch)
            probs_T(B * PAIRS - 1, 1)
            add_z(B - 1, 1)
            groups(dve, [(3, g_stats(SPEC2)), (2, g_norm(SPEC2)), (0, add_bank(mm_done, 4 * G, lambda j: BANK_OUT + j))])

        @block.scalar
        def _(act):
            for dst, src in ((w123_s[:, 0, :], W1), (w123_s[:, 1, :], W2), (w123_s[:, 2, :], W3), (wd_s[:], Wd),
                             (wu_s[:], Wu), (wre_s[:], w_re), (wim_s[:], w_im),
                             (dft_s[:].rearrange("p a d -> p (a d)"), dft), (wq_s[:], Wq), (wo_s[:], Wo),
                             (bd_s[:], bd.unsqueeze(1)), (rows[:, BQ:BQ + D], bq.unsqueeze(0)),
                             (rows[:, BFFN:BFFN + D], ffn_bias.unsqueeze(0)), (rows[:, BFFT:BFFT + D], fft_bias.unsqueeze(0)),
                             (rows[:, BO:BO + D], bo.unsqueeze(0)), (rows[:, BU:BU + 2 * D], bu.unsqueeze(0))):
                act.dma_start(dst, src).then_inc(in_small, 16)
            act.wait_ge(su_pe, 1)
            nc.scalar.copy(wt_s[:, 0:2, :].rearrange("p a d -> p (a d)"), ps[:, 0, 0:2 * D])
            nc.scalar.copy(wt_s[0:R, 2, :], ps[0:R, 0, 2 * D:3 * D]).then_inc(su_ev, 1)
            act.wait_ge(su_pe, 2)
            nc.scalar.copy(abT[:, 0, :], ps[:, 1, 0:D])
            nc.scalar.mul(abT[:, 1, :], ps[:, 2, 0:D], -1.0).then_inc(su_ev, 1)
            act.wait_ge(su_pe, 3)
            nc.scalar.copy(w23[:], ps[:, 3, 0:D])
            nc.scalar.copy(wkv[:], ps[:, 3, D:3 * D]).then_inc(su_ev, 1)
            act.wait_ge(su_pe, 4)
            nc.scalar.copy(wc[:], ps[:, 5, 0:D])
            nc.scalar.mul(circ[:], ps[:, 6, 0:D], 0.5 / D).then_inc(su_ev, 1)
            for i in range(4):
                act.wait_ge(su_pe, count(5 + i))
                nc.scalar.mul(g_hi[:, 4 * i:4 * i + 4, :].rearrange("p h d -> p (h d)"), ps[:, i, :], SCORE_SCALE).then_inc(su_hi, 1)
            for i in range(2):
                act.wait_ge(su_pe, count(9 + i))
                nc.scalar.copy(v_hi[:, 512 * i:512 * i + 512], ps[:, 4 + i, :]).then_inc(su_hi, 1)
            for i in range(2):
                act.wait_ge(su_pe, count(11 + i))
                nc.scalar.mul(wz[:, 4 * i:4 * i + 4, :].rearrange("p h d -> p (h d)"), ps[:, 6 + i, :], OUT_SCALE).then_inc(su_ev, 1)

            def xT_out(phase):
                def f(g, j):
                    act.wait_ge(tr_done, count(ln_no(phase, g) + 1))
                    if phase == LIN and (isinstance(g, Count) or g >= 2):
                        act.wait_ge(q_done, count(g - 1))
                        act.wait_ge(kv_done, count(g - 1))
                    else:
                        if above_0(g + (phase * G - 1)):
                            act.wait_ge(mm_done, count(g + (phase * G - 1)))
                    nc.scalar.copy(xT[:, j, :], ps[:, 0 if phase == LIN else j, :]).then_inc(xT_ready, 1)
                return f

            def tanh(phase, k):
                def f(g, j):
                    act.wait_ge(mm_done, count(g + (phase * G + 1)))
                    if above_0(g + (phase * G - 1)):
                        act.wait_ge(x_ready, count(g + (phase * G - 1)))
                    nc.scalar.activation(th[:, j, :], ps[:, BANK_OUT + j, :], ACT.Tanh).then_inc(th_ready, 1)
                return f

            def exp_k(g, j):
                act.wait_ge(kv_done, count(g + 1))
                if above_0(2 * g - 1):
                    act.wait_ge(phi_ready, count(2 * g - 1))
                nc.scalar.activation(ek[:], kv[:, :, 0:P], ACT.Exp, bias=-1.0).then_inc(ek_ready, 1)
                if above_0(g):
                    act.wait_ge(ctx_done, count(g))
                nc.scalar.copy(vones[:, :, 0:P], kv[:, :, P:2 * P]).then_inc(v0_ready, 1)

            def exp_q(g, j):
                act.wait_ge(q_done, count(g + 1))
                if above_0(2 * g):
                    act.wait_ge(phi_ready, count(2 * g))
                nc.scalar.activation(eq[:], ps[:, LIN_Q, :], ACT.Exp, bias=-1.0).then_inc(eq_ready, 1)

            def denominator(g, j):
                act.wait_ge(nd_done, count(g + 1))
                if above_0(g):
                    act.wait_ge(y0_ready, count(g))
                nc.scalar.activation(zr[:], ps[:, LIN_D, :], ACT.Identity, bias=Z_EPS).then_inc(den_ready, 1)

            groups(act, [(1, xT_out(FFN1)), (0, tanh(FFN1, 0))])
            groups(act, [(1, exp_q), (1, exp_k), (0, denominator), (2, xT_out(LIN))])
            groups(act, [(1, xT_out(FFN2)), (0, tanh(FFN2, 1))])
            groups(act, [(1, xT_out(SPEC1))])

            def x_high(b, j):
                act.wait_ge(tr_done, count(b + (LN_SOFT + 1)))
                if above_0(2 * PAIRS * (b - 1)):
                    act.wait_ge(s_done, count(2 * PAIRS * (b - 1)))
                nc.scalar.copy(x_hi[:, j, :], ps[:, BANK_X, 0:T]).then_inc(xhi_ready, 1)

            def u_high(n, j):
                act.wait_ge(u_done, count(n + 1))
                if above_0(2 * n - 2):
                    act.wait_ge(s_done, count(2 * n - 2))
                nc.scalar.copy(u_hi[:, j].rearrange("p h k -> p (h k)"), ps[:, BANK_U, :]).then_inc(uhi_ready, 1)

            def exp_tile(n, j, qt):
                act.wait_ge(max_ready, count(2 * n + (1 + qt)))
                if qt == 0:
                    if above_0(n - 1):
                        act.wait_ge(pt_done, count(n - 1))
                    if above_0(n - 1):
                        act.wait_ge(rinv_ready, count(n - 1))
                w = (qt + 1) * P
                for h in range(2):
                    at = 2 * h + qt
                    dst = pr[:, j, h, 0, :] if qt == 0 else pr[:, j, h, 1:3, :].rearrange("p b k -> p (b k)")
                    last = nc.scalar.activation(dst, ps[:, BANK_S + 2 * j + qt, h * w:(h + 1) * w], ACT.Exp,
                                                bias=nmax[:, j, at:at + 1], accum_out=rsum[:, j, at:at + 1])
                last.then_inc(exp_ready, 1)

            def probs_T(n, j):
                act.wait_ge(pt_done, count(n + 1))
                if above_0(n - 1):
                    act.wait_ge(pv_done, count(n - 1))
                nc.scalar.copy(pT[:, j].rearrange("p h b q -> p (h b q)")[:, 512:768], ps[:, BANK_T + 1, 0:256]).then_inc(pTb_ready, 1)

            def values_out(b, j, c):
                act.wait_ge(v_done, count(4 * b + (c + 1)))
                if c == 0:
                    if above_0(PAIRS * (b - 1)):
                        act.wait_ge(pv_done, count(PAIRS * (b - 1)))
                nc.scalar.copy(vv[:, j, c % 2, 512 * (c // 2):512 * (c // 2) + 512], ps[:, BANK_X, :]).then_inc(v_ready, 1)

            def y_out(b, jb, p):
                act.wait_ge(pv_done, count(b * PAIRS + (p + 1)))
                if p == 0:
                    if above_0(b - 1):
                        act.wait_ge(w_done, count(b - 1))
                nc.scalar.copy(yT[:, jb, p, :], y_bank).then_inc(y_ready, 1)

            x_high(0, 0)
            u_high(0, 0)
            u_high(1, 1)
            u_high(2, 0)
            exp_tile(0, 0, 0)
            exp_tile(0, 0, 1)
            for c in range(4):
                values_out(0, 0, c)

            def batch(b, jb, first=False, last=False):
                for p in range(PAIRS):
                    n, j = b * PAIRS + p, p % 2
                    if not (first and p == 0):
                        probs_T(n - 1, 1 - j)
                    if not (last and p >= PAIRS - 3):
                        u_high(n + 3, 1 - j)
                    if not (last and p >= PAIRS - 1):
                        exp_tile(n + 1, 1 - j, 0)
                    if p > 0:
                        y_out(b, jb, p - 1)
                    elif not first:
                        y_out(b - 1, 1 - jb, PAIRS - 1)
                    if not (last and p >= PAIRS - 1):
                        exp_tile(n + 1, 1 - j, 1)
                    if p == 2 and not last:
                        x_high(b + 1, 1 - jb)
                    if p >= V_TURN and not last:
                        values_out(b + 1, 1 - jb, p - V_TURN)

            batches(act, batch)
            probs_T(B * PAIRS - 1, 1)
            y_out(B - 1, 1, PAIRS - 1)
            groups(act, [(1, xT_out(SPEC2))])

        @block.tensor
        def _(pe):
            mm, tr = nc.tensor.matmul, nc.tensor.transpose
            wu_kv = wu_s[:].rearrange("r (h s e) -> r s h e", s=2, e=E0)
            pe.wait_ge(pool_const, 3)
            pe.wait_ge(in_small, 16 * SMALL_LOADS)
            tr(ps[:, 0, 0:D], w123_s[:, 0, :], ident[:])
            tr(ps[:, 0, D:2 * D], w123_s[:, 1, :], ident[:])
            tr(ps[0:R, 0, 2 * D:3 * D], wd_s[:], ident[:]).then_inc(su_pe, 1)
            cos, sin, nsin = (dft_s[:, k, :] for k in range(3))
            mm(ps[:, 1, 0:D], wre_s[:], cos, start=True, stop=False, skip_group_check=True)
            mm(ps[:, 1, 0:D], wim_s[:], sin, start=False, stop=True, skip_group_check=True)
            mm(ps[:, 2, 0:D], wim_s[:], cos, start=True, stop=False, skip_group_check=True)
            mm(ps[:, 2, 0:D], wre_s[:], nsin, start=False, stop=True, skip_group_check=True).then_inc(su_pe, 1)
            pe.wait_ge(su_ev, 1)
            mm(ps[:, 3, 0:D], wt_s[:, 1, :], w123_s[:, 2, :], start=True, stop=True)
            for s in range(2):
                mm(ps[:, 3, (1 + s) * D:(2 + s) * D], wt_s[0:R, 2, :], wu_kv[:, s], start=True, stop=True)
            for s in range(2):
                last = mm(ps[0:1, 4, s * D:(s + 1) * D], bd_s[:], wu_kv[:, s], start=True, stop=True)
            last.then_inc(su_pe, 1)
            pe.wait_ge(su_ev, 3)
            mm(ps[:, 5, 0:D], wt_s[:, 0, :], w23[:], start=True, stop=True)
            mm(ps[:, 6, 0:D], abT[:, 0, :], cos, start=True, stop=False, skip_group_check=True)
            mm(ps[:, 6, 0:D], abT[:, 1, :], sin, start=False, stop=True, skip_group_check=True).then_inc(su_pe, 1)
            pe.wait_ge(in_qk, 32)
            q_h = q_raw.rearrange("q (d h) -> q h d", h=H)
            k_h = k_raw.rearrange("q (d h) -> q h d", h=H)
            for h in range(H):
                last = mm(ps[:, h // 4, (h % 4) * D:(h % 4 + 1) * D], k_h[:, h, :], q_h[:, h, :], start=True, stop=True)
                if h % 4 == 3:
                    last.then_inc(su_pe, 1)
            pe.wait_ge(in_vw, 32)
            pe.wait_ge(su_ev, 4)
            pe.wait_ge(su_row, 6)
            v_h = v_raw.rearrange("v (d h) -> v h d", h=H)
            for h in range(H):
                last = tr(ps[:, 4 + h // 8, (h % 8) * DV:(h % 8 + 1) * DV], v_h[:, h, :], ident[0:DV, 0:DV])
                if h % 8 == 7:
                    last.then_inc(su_pe, 1)
            pe.wait_ge(w_heads_ready, 1)
            for p in range(PAIRS):
                last = tr(ps[:, 6 + p // 4, (p % 4) * D:(p % 4 + 1) * D], w_heads[:, p * P:(p + 1) * P], ident[:])
                if p % 4 == 3:
                    last.then_inc(su_pe, 1)
            pe.wait_ge(su_lo, 6)
            pe.wait_ge(su_ev, 6)
            pe.wait_ge(su_x, 1)

            def transpose(phase):
                def f(g, j):
                    n = g + phase * G
                    pe.wait_ge(xn_ready, count(ln_no(phase, g) + 1))
                    if phase == LIN or g == 0:
                        if above_0(n):
                            pe.wait_ge(xT_ready, count(n))
                    else:
                        if above_0(n - 1):
                            pe.wait_ge(xT_ready, count(n - 1))
                    if g == 1:
                        if above_0(X_BEFORE[phase]):
                            pe.wait_ge(x_ready, count(X_BEFORE[phase]))
                    for t in range(GT):
                        last = tr(ps[:, 0 if phase == LIN else j, t * P:(t + 1) * P], xn[:, j, t * D:(t + 1) * D], ident[:])
                    last.then_inc(tr_done, 1)
                return f

            def product(phase, w, bias, freed, before):
                def f(g, j):
                    pe.wait_ge(xT_ready, count(g + (phase * G + 1)))
                    if above_0(g + (before - 1)):
                        pe.wait_ge(freed, count(g + (before - 1)))
                    bank = ps[:, BANK_OUT + j, :]
                    mm(bank, ones_bf[:, 0:P], bias_bf[:, bias, :], start=True, stop=False, skip_group_check=True)
                    for t in range(GT):
                        last = mm(bank[:, t * D:(t + 1) * D], xT[:, j, t * P:(t + 1) * P], w, start=False, stop=True,
                                  skip_group_check=True)
                    last.then_inc(mm_done, 1)
                return f

            groups(pe, [(1, transpose(FFN1)), (0, product(FFN1, wc[:], FFN_B, th_ready, 0))])

            def lin_project(g, j):
                if g == 0:
                    pe.wait_ge(x_ready, G)
                pe.wait_ge(xT_ready, count(g + (G + 1)))
                if above_0(2 * g):
                    pe.wait_ge(phi_ready, count(2 * g))
                if above_0(g):
                    pe.wait_ge(v0_ready, count(g))
                mm(ps[:, LIN_Q, :], biasq_bf[:], ones_bf[:], start=True, stop=False, skip_group_check=True)
                mm(ps[:, LIN_Q, :], wq_s[:], xT[:, j, :], start=False, stop=True, skip_group_check=True).then_inc(q_done, 1)
                for k in range(2):
                    bank = ps[:, LIN_KV + k, :]
                    mm(bank, ones_bf[:, 0:P], bias_bf[:, KV_B, :], start=True, stop=False, skip_group_check=True)
                    for t in range(2):
                        last = mm(bank[:, t * 2 * D:(t + 1) * 2 * D], xT[:, j, (2 * k + t) * P:(2 * k + t + 1) * P],
                                  wkv[:], start=False, stop=True, skip_group_check=True)
                last.then_inc(kv_done, 1)

            def lin_context(g, j):
                pe.wait_ge(phi_ready, count(2 * g + 1))
                if above_0(g):
                    pe.wait_ge(cbd_ready, count(g))
                for b in range(GB):
                    for t in range(BT):
                        last = mm(ps[:, LIN_C, b * 2 * P:(b + 1) * 2 * P], phk[:, b * BT + t, :], vones[:, b * BT + t, :],
                                  start=(t == 0), stop=(t == BT - 1))
                last.then_inc(ctx_done, 1)

            def lin_outputs(g, j):
                pe.wait_ge(cbd_ready, count(g + 1))
                pe.wait_ge(phi_ready, count(2 * g + 2))
                if above_0(g):
                    pe.wait_ge(y0_ready, count(g))
                for bank, at in ((LIN_D, P), (LIN_N, 0)):
                    for b in range(GB):
                        last = mm(ps[:, bank, b * T:(b + 1) * T], cbd[:, b, at:at + P], phq[:, j, b * T:(b + 1) * T],
                                  start=True, stop=True)
                last.then_inc(nd_done, 1)

            def lin_project_out(g, j):
                pe.wait_ge(y0_ready, count(g + 1))
                pe.wait_ge(x_ready, count(g + G))
                mm(ps[:, LIN_O, :], ones_bf[:, 0:P], bias_bf[:, BO_B, :], start=True, stop=False, skip_group_check=True)
                for t in range(GT):
                    last = mm(ps[:, LIN_O, t * D:(t + 1) * D], yT0[:, t * P:(t + 1) * P], wo_s[:], start=False, stop=True,
                              skip_group_check=True)
                last.then_inc(mm_done, 1)

            groups(pe, [(1, lin_project), (0, lin_outputs), (2, transpose(LIN)), (1, lin_context), (0, lin_project_out)])
            groups(pe, [(1, transpose(FFN2)), (0, product(FFN2, wc[:], FFN_B, th_ready, G))])
            groups(pe, [(1, transpose(SPEC1)), (0, product(SPEC1, circ[:], FFT_B, x_ready, 3 * G))])

            def x_transpose(b, j):
                pe.wait_ge(xn_ready, count(b + (LN_SOFT + 1)))
                for t in range(BT):
                    last = tr(ps[:, BANK_X, t * P:(t + 1) * P], xn[:, j, t * D:(t + 1) * D], ident[:])
                last.then_inc(tr_done, 1)

            def u_product(n, h2, jb, j):
                for k in range(2):
                    h = 2 * h2 + k
                    o = ps[:, BANK_U, k * T:(k + 1) * T]
                    mm(o, g_hi[:, h, :], x_hi[:, jb, :], start=True, stop=False, skip_group_check=True)
                    mm(o, g_hi[:, h, :], x_lo[:, jb, :], start=False, stop=False, skip_group_check=True)
                    last = mm(o, g_lo[:, h, :], x_hi[:, jb, :], start=False, stop=True, skip_group_check=True)
                last.then_inc(u_done, 1)

            def scores(n, jb, j):
                pe.wait_ge(ulo_ready, count(n + 1))
                if above_0(2 * n - 3):
                    pe.wait_ge(exp_ready, count(2 * n - 3))
                o = ps[:, BANK_S + 2 * j, 0:2 * P].rearrange("p (h k) -> p h k", h=2)
                uh, ul = (a[:, j, :, 0:P] for a in (u_hi, u_lo))
                xh, xl = x_hi[:, jb, 0:P], x_lo[:, jb, 0:P]
                mm(o, ident_bf[:], mask_bf[:], start=True, stop=False, skip_group_check=True)
                mm(o, xh, uh, start=False, stop=False, skip_group_check=True)
                mm(o, xh, ul, start=False, stop=False, skip_group_check=True)
                mm(o, xl, uh, start=False, stop=True, skip_group_check=True).then_inc(s_done, 1)
                if above_0(2 * n - 2):
                    pe.wait_ge(exp_ready, count(2 * n - 2))
                o = ps[:, BANK_S + 2 * j + 1, :].rearrange("p (h k) -> p h k", h=2)
                uh, ul = u_hi[:, j], u_lo[:, j]
                xh, xl = x_hi[:, jb, P:2 * P], x_lo[:, jb, P:2 * P]
                mm(o, xh, uh, start=True, stop=False, skip_group_check=True)
                mm(o[:, :, P:2 * P], ident_bf[:], mask_bf[:], start=False, stop=False, skip_group_check=True)
                mm(o, xh, ul, start=False, stop=False, skip_group_check=True)
                mm(o, xl, uh, start=False, stop=True, skip_group_check=True).then_inc(s_done, 1)

            def probs_transpose(n, j):
                pe.wait_ge(pn_ready, count(n + 1))
                if above_0(n):
                    pe.wait_ge(pTa_ready, count(n))
                for k in range(6):
                    if k == 4 and above_0(n):
                        pe.wait_ge(pTb_ready, count(n))
                        pe.wait_ge(y_ready, count(n))
                    last = tr(ps[:, BANK_T + k // 4, (k % 4) * P:(k % 4 + 1) * P], pr[:, j, k // 3, k % 3, :], ident[:])
                last.then_inc(pt_done, 1)

            def values(b, j, c):
                at = slice(512 * (c // 2), 512 * (c // 2) + 512)
                tok = slice((c % 2) * P, (c % 2 + 1) * P)
                mm(ps[:, BANK_X, :], x_hi[:, j, tok], v_hi[:, at], start=True, stop=False, skip_group_check=True)
                mm(ps[:, BANK_X, :], x_hi[:, j, tok], v_lo[:, at], start=False, stop=False, skip_group_check=True)
                mm(ps[:, BANK_X, :], x_lo[:, j, tok], v_hi[:, at], start=False, stop=True, skip_group_check=True).then_inc(v_done, 1)

            def products(n, p, jb, j):
                pe.wait_ge(pTa_ready, count(n + 1))
                pe.wait_ge(pTb_ready, count(n + 1))
                for kt in range(BT):
                    for k in range(2):
                        h = 2 * p + k
                        last = mm(y_bank[k * DV:(k + 1) * DV, kt * P:T], vv[:, jb, kt, h * DV:(h + 1) * DV],
                                  pT[:, j, k, 0:2, :] if kt == 0 else pT[:, j, k, 2, :], start=(kt == 0), stop=(kt == 1),
                                  skip_group_check=True)
                last.then_inc(pv_done, 1)

            def project_out(b, j):
                pe.wait_ge(y_ready, count(PAIRS * (b + 1)))
                for t in range(BT):
                    for p in range(PAIRS):
                        last = mm(ps[:, BANK_X, t * D:(t + 1) * D], yT[:, j, p, t * P:(t + 1) * P], wz[:, p, :],
                                  start=(p == 0), stop=(p == PAIRS - 1))
                last.then_inc(w_done, 1)

            pe.wait_ge(x_ready, 4 * G)
            x_transpose(0, 0)
            pe.wait_ge(xlo_ready, 1)
            u_product(0, 0, 0, 0)
            pe.wait_ge(ulo_ready, 1)
            u_product(1, 1, 0, 1)
            scores(0, 0, 0)
            pe.wait_ge(ulo_ready, 2)
            u_product(2, 2, 0, 0)
            scores(1, 0, 1)
            values(0, 0, 0)
            for c in range(1, 4):
                pe.wait_ge(v_ready, c)
                values(0, 0, c)

            def batch(b, jb, first=False, last=False):
                for p in range(PAIRS):
                    n, j = b * PAIRS + p, p % 2
                    if not (last and p >= PAIRS - 3):
                        pe.wait_ge(ulo_ready, count(n + 3))
                        u_product(n + 3, (p + 3) % PAIRS, jb if p + 3 < PAIRS else 1 - jb, 1 - j)
                    if not (last and p >= PAIRS - 2):
                        scores(n + 2, jb if p + 2 < PAIRS else 1 - jb, j)
                    if p > 0:
                        products(n - 1, p - 1, jb, 1 - j)
                    elif not first:
                        products(n - 1, PAIRS - 1, 1 - jb, 1 - j)
                    if p == 1 and not first:
                        pe.wait_ge(v_ready, count(4 * (b + 1)))
                        project_out(b - 1, 1 - jb)
                    if p == 2 and not last:
                        if first:
                            pe.wait_ge(v_ready, 4)
                        else:
                            pe.wait_ge(x_ready, count(b + X_SOFT))
                        x_transpose(b + 1, 1 - jb)
                    if p == V_TURN and not last:
                        pe.wait_ge(xlo_ready, count(b + 2))
                    if p > V_TURN and not last:
                        pe.wait_ge(v_ready, count(4 * (b + 1) + (p - V_TURN)))
                    if p >= V_TURN and not last:
                        values(b + 1, 1 - jb, p - V_TURN)
                    probs_transpose(n, j)

            batches(pe, batch)
            products(B * PAIRS - 1, PAIRS - 1, 1, 1)
            pe.wait_ge(x_ready, X_SOFT + B - 1)
            project_out(B - 1, 1)
            groups(pe, [(1, transpose(SPEC2)),
                        (0, product(SPEC2, circ[:], FFT_B, x_ready, X_BEFORE[SPEC2]))])


_INS = ["L0_attn_x", "L0_attn_Wq", "L0_attn_bq", "L0_attn_Wd", "L0_attn_bd", "L0_attn_Wu", "L0_attn_bu",
        "L0_attn_Wo", "L0_attn_bo", "L0_ffn_weight", "L0_ffn_aux_weight1", "L0_ffn_aux_weight2", "L0_ffn_bias",
        "L1_attn_Q", "L1_attn_K", "L1_attn_V", "L1_attn_W", "L1_ffn_w_freq_real", "L1_ffn_w_freq_imag", "L1_ffn_bias"]


def dft_tables():
    a = 2 * np.pi / D * (np.arange(D)[:, None] * np.arange(D)[None, :] % D)
    return np.concatenate([np.cos(a), np.sin(a), -np.sin(a)], axis=1).astype(np.float32)


def kernel(**inputs):
    import concourse.bacc as bacc
    from concourse.bass_utils import run_bass_kernel_spmd

    nc = bacc.Bacc("TRN2", target_bir_lowering=False, num_devices=1)
    arrays, args = {}, []
    for name in _INS:
        a = np.ascontiguousarray(inputs[name])
        arrays[name] = a
        args.append(nc.dram_tensor(name, a.shape, mybir.dt.from_np(a.dtype), kind="ExternalInput").ap())
    arrays["dft"] = dft_tables()
    args.append(nc.dram_tensor("dft", (D, 3 * D), F32, kind="ExternalInput").ap())
    args.append(nc.dram_tensor("out", (B, T, D), F32, kind="ExternalOutput").ap())
    build(nc, *args)
    r = run_bass_kernel_spmd(nc, [arrays], core_ids=[0])
    return r.results[0]["out"]
```

```python
import concourse.bass as bass
import numpy as np
from concourse import mybir
from contextlib import ExitStack

F32 = mybir.dt.float32
F32R = mybir.dt.float32r
BF16 = mybir.dt.bfloat16
ALU = mybir.AluOpType
ACT = mybir.ActivationFunctionType
AX = mybir.AxisListType

B, T, D = 32, 256, 128
P = 128
TILES = B * T // P
BT = T // P
G = 16
GT = TILES // G
GB = B // G
GW = GT * D
H0, R = 16, 32
E0 = D // H0
H, DQ, DV = 16, 64, 64
PAIRS = H // 2
EPS = 1e-5
Z_EPS = 1e-6
MASKED = -3.0e38
SCORE_SCALE = 1.0 / D
OUT_SCALE = 1.0 / H
LEAD = 4


class Count:

    def __init__(self, i, step=1, base=0):
        self.i, self.step, self.base = i, step, base

    def __add__(self, n):
        return Count(self.i, self.step, self.base + n)

    __radd__ = __add__

    def __sub__(self, n):
        return self + -n

    def __mul__(self, n):
        return Count(self.i, self.step * n, self.base * n)

    __rmul__ = __mul__


def count(n):
    return n.i * n.step + n.base if isinstance(n, Count) else n


def phases(eng, plan):
    def turn(stages, t):
        for lead, f in stages:
            if 0 <= t + lead < G:
                f(t + lead, (t + lead) % 2)
    last = (G - LEAD) // 2
    before = []
    for stages in plan:
        for t in range(-LEAD, 2):
            if t < 0:
                turn(before, G + t)
            turn(stages, t)
        with eng.Fori(1, last) as i:
            for j in range(2):
                for lead, f in stages:
                    f(Count(i, 2, j + lead), (j + lead) % 2)
        for t in range(2 * last, G - LEAD):
            turn(stages, t)
        before = stages
    for t in range(G - LEAD, G):
        turn(before, t)


def batches(eng, batch):
    batch(0, 0, first=True)
    batch(1, 1)
    with eng.Fori(1, B // 2 - 1) as i:
        for j in range(2):
            batch(Count(i, 2, j), j)
    batch(B - 2, 0)
    batch(B - 1, 1, last=True)


def above_0(n):
    return isinstance(n, Count) or n > 0


def build(nc, x, Wq, bq, Wd, bd, Wu, bu, Wo, bo, W1, W2, W3, ffn_bias, Q, K, V, W, w_re, w_im, fft_bias, dft, out):
    ctx = ExitStack()
    with ctx:
        def sb(name, shape, dt=F32):
            return ctx.enter_context(nc.sbuf_tensor(name, shape, dt))

        def sem(name):
            return ctx.enter_context(nc.semaphore(name))

        x_all = sb("x_all", [P, TILES * D])
        ident = sb("ident", [P, P])
        mask = sb("mask", [P, T])
        ones_bf = sb("ones_bf", [P, 512], BF16)
        head_mask = sb("head_mask", [P, GB, P])
        wq_s = sb("wq_s", [P, D]); wd_s = sb("wd_s", [P, R]); wu_s = sb("wu_s", [R, 2 * D])
        bd_s = sb("bd_s", [R, 1]); wo_s = sb("wo_s", [P, D])
        w123_s = sb("w123_s", [P, 3, D]); wre_s = sb("wre_s", [P, D]); wim_s = sb("wim_s", [P, D])
        dft_s = sb("dft_s", [P, 3, D])
        rows = sb("rows", [1, 4 * D + 2 * D])
        BQ, BFFN, BFFT, BO, BU = 0, D, 2 * D, 3 * D, 4 * D
        space = sb("space", [P, 2 * BT * H * DV + 2 * PAIRS * T])
        q_raw, k_raw, v_raw = (space[0:DQ, k * D * H:(k + 1) * D * H] for k in range(3))
        w_raw = space[:, 3 * D * H:3 * D * H + DV * H]
        w_heads = space[:, 3 * D * H + DV * H:3 * D * H + 2 * DV * H]
        wt_s = sb("wt_s", [P, 3, D])
        w23 = sb("w23", [P, D]); wc = sb("wc", [P, D])
        wkv = sb("wkv", [P, 2 * D])
        abT = sb("abT", [P, 2, D]); circ = sb("circ", [P, D])
        bias_bf = sb("bias_bf", [P, 4, 512], BF16)
        biasq_bf = sb("biasq_bf", [P, P], BF16)
        FFN_B, FFT_B, BO_B, KV_B = range(4)
        kvrow = sb("kvrow", [1, 2 * D])
        rest = sb("rest", [1, 2, 512])
        bwide = sb("bwide", [1, 5, 512])
        g_hi = sb("g_hi", [P, H, D], F32R); g_lo = sb("g_lo", [P, H, D], F32R)
        v_hi = sb("v_hi", [P, H * DV], F32R); v_lo = sb("v_lo", [P, H * DV], F32R)
        wz = sb("wz", [P, PAIRS, D])
        half_neg = sb("half_neg", [P, GT]); eps_t = sb("eps_t", [P, GT])
        bst = sb("bst", [P, 2, GT, 6]); mv = sb("mv", [P, 2, GT, 2])
        veps = sb("veps", [P, 2, GT]); rstd = sb("rstd", [P, 2, GT]); minus_1 = sb("minus_1", [P, GT])
        neg_mean = sb("neg_mean", [P, 2, GT]); shift = sb("shift", [P, 2, GT])
        act_pause = sb("act_pause", [P, 2])
        pause = sb("pause", [P, 5])
        xn = sb("xn", [P, 2, GW])
        xT = sb("xT", [P, 2, GW])
        th = sb("th", [P, 2, GW])
        eq = sb("eq", [P, GW]); ek = sb("ek", [P, GT, P])
        phq = sb("phq", [P, 2, GW]); phk = sb("phk", [P, GT, P])
        vones = sb("vones", [P, GT, P + 1])
        cbd = sb("cbd", [P, GB, P + H0])
        den = sb("den", [P, GT, H0]); zr = sb("zr", [P, GT, H0])
        y0 = sb("y0", [P, GT, P]); yT0 = sb("yT0", [P, GW])
        x_hi = sb("x_hi", [P, 2, T], F32R); x_lo = sb("x_lo", [P, 2, T], F32R)
        u_hi = sb("u_hi", [P, 2, 2, T], F32R); u_lo = sb("u_lo", [P, 2, 2, T], F32R)
        neg_max = sb("neg_max", [P, 2, 4]); rsum = sb("rsum", [P, 2, 4]); rinv = sb("rinv", [P, 2, 4])
        pr = sb("pr", [P, 2, 2, 3, P])
        pT = sb("pT", [P, 2, 2, 3, P])
        vv = space[:, 0:2 * BT * H * DV].rearrange("p (r t n) -> p r t n", r=2, t=BT)
        yT = space[:, 2 * BT * H * DV:].rearrange("p (r a t) -> p r a t", r=2, a=PAIRS)

        ps = ctx.enter_context(nc.psum_tensor("ps", [P, 8, 512], F32))

        in_first = sem("in_first"); in_rest = sem("in_rest")
        in_small = sem("in_small"); in_qk = sem("in_qk"); in_vw = sem("in_vw")
        pool_const = sem("pool_const");
        su_pe = sem("su_pe"); su_ev = sem("su_ev"); su_row = sem("su_row"); su_x = sem("su_x")
        su_hi = sem("su_hi"); su_lo = sem("su_lo"); w_heads_ready = sem("w_heads_ready")
        stats_done = sem("stats_done"); mv_ready = sem("mv_ready")
        pool_step = sem("pool_step"); rstd_ready = sem("rstd_ready")
        shift_ready = sem("shift_ready"); neg_mean_ready = sem("neg_mean_ready")
        xn_ready = sem("xn_ready"); xn_act_ready = sem("xn_act_ready"); tr_done = sem("tr_done"); xT_ready = sem("xT_ready")
        mm_done = sem("mm_done"); th_ready = sem("th_ready"); x_ready = sem("x_ready")
        q_done = sem("q_done"); kv_done = sem("kv_done"); ek_ready = sem("ek_ready"); eq_ready = sem("eq_ready"); v0_ready = sem("v0_ready"); phi_ready = sem("phi_ready")
        ctx_done = sem("ctx_done"); cbd_ready = sem("cbd_ready"); nd_done = sem("nd_done")
        den_ready = sem("den_ready"); zr_ready = sem("zr_ready"); y0_ready = sem("y0_ready"); y0t_done = sem("y0t_done"); yT0_ready = sem("yT0_ready")
        u_done = sem("u_done"); uhi_ready = sem("uhi_ready"); ulo_ready = sem("ulo_ready")
        s_done = sem("s_done"); max_ready = sem("max_ready"); exp_ready = sem("exp_ready")
        rinv_ready = sem("rinv_ready"); pn_ready = sem("pn_ready"); pt_done = sem("pt_done")
        pTa_ready = sem("pTa_ready"); pTb_ready = sem("pTb_ready")
        pv_done = sem("pv_done"); y_ready = sem("y_ready")
        v_done = sem("v_done"); v_ready = sem("v_ready"); w_done = sem("w_done")
        xhi_ready = sem("xhi_ready"); xlo_ready = sem("xlo_ready")
        out_done = sem("out_done")

        block = ctx.enter_context(nc.Block())
        SMALL_LOADS = 16

        def xg(g, t=0, n=GT):
            return x_all[:, bass.ds(count(g * GW + t * D), n * D)]

        def xb(b, t=0, n=BT):
            return x_all[:, bass.ds(count(b * (BT * D) + t * D), n * D)]

        LIN_Q, LIN_KV, LIN_C, LIN_N, LIN_O = 1, 2, 4, 5, 7
        kv = ps[:, LIN_KV:LIN_KV + 2, :].rearrange("p b (t n) -> p (b t) n", n=2 * P)
        num_den = ps[:, LIN_N:LIN_N + 2, :].rearrange("p b (t n) -> p (b t) n", n=2 * P)
        BANK_OUT = 5
        BANK_U, BANK_S, BANK_X, BANK_T = 0, 1, 5, 6
        y_bank = ps[:, BANK_T + 1, 512 - T:512]

        FFN1, LIN, FFN2, SPEC1, SPEC2 = range(5)
        X_BEFORE = {FFN1: 0, LIN: G, FFN2: 2 * G, SPEC1: 3 * G, SPEC2: 4 * G + B}
        X_SOFT = 4 * G
        LN_SOFT = 4 * G

        def ln_no(phase, g):
            return g + (phase * G if phase < SPEC2 else LN_SOFT + B)

        ACT_TILES = 2

        def act_no(phase, n):
            return n - B if phase == SPEC2 else n

        V_TURN = 4

        @block.sync
        def _(sp):
            def tiles_of(a, b0, b1):
                return a[b0:b1].rearrange("b (t p) d -> p (b t) d", p=P)
            sp.dma_start(x_all[:, 0:2 * GW].rearrange("p (t d) -> p t d", d=D), tiles_of(x, 0, 2 * GB)).then_inc(in_first, 16)
            sp.dma_start(x_all[:, 2 * GW:].rearrange("p (t d) -> p t d", d=D), tiles_of(x, 2 * GB, B)).then_inc(in_rest, 16)
            sp.dma_start(q_raw, Q.rearrange("q d h -> q (d h)")).then_inc(in_qk, 16)
            sp.dma_start(k_raw, K.rearrange("q d h -> q (d h)")).then_inc(in_qk, 16)
            sp.dma_start(v_raw, V.rearrange("q d h -> q (d h)")).then_inc(in_vw, 16)
            sp.dma_start(w_raw, W.rearrange("d v h -> d (v h)")).then_inc(in_vw, 16)
            with sp.Fori(0, G) as i:
                g = Count(i)
                sp.wait_ge(x_ready, count(g + (X_BEFORE[SPEC2] + 1)))
                sp.dma_start(out[bass.ds(count(g * GB), GB)].rearrange("b (t p) d -> p (b t) d", p=P),
                             xg(g).rearrange("p (t d) -> p t d", d=D)).then_inc(out_done, 16)
            sp.wait_ge(out_done, 16 * G)

        @block.gpsimd
        def _(pool):
            nc.gpsimd.memset(ident[:], 0.0).then_inc(pool_step, 1)
            nc.gpsimd.memset(mask[:], 0.0).then_inc(pool_step, 1)
            nc.gpsimd.memset(head_mask[:], 1.0).then_inc(pool_step, 1)
            nc.gpsimd.memset(half_neg[:], -0.5)
            nc.gpsimd.memset(eps_t[:], EPS)
            nc.gpsimd.memset(minus_1[:], -1.0)
            nc.gpsimd.memset(ones_bf[:], 1.0)
            nc.gpsimd.memset(vones[:], 1.0)
            pool.wait_ge(pool_step, 3)
            nc.gpsimd.affine_select(out=ident[:], in_=ident[:], compare_op=ALU.not_equal, fill=1.0, base=0,
                                    pattern=[[-1, P]], channel_multiplier=1).then_inc(pool_const, 1)
            nc.gpsimd.affine_select(out=mask[:], in_=mask[:], compare_op=ALU.is_ge, fill=MASKED, base=P,
                                    pattern=[[-1, T]], channel_multiplier=1).then_inc(pool_const, 1)
            hm = head_mask[:].rearrange("p a (h e) -> p (a h) e", e=E0)
            nc.gpsimd.affine_select(out=hm, in_=hm, compare_op=ALU.is_ge, fill=0.0, base=0,
                                    pattern=[[0, GB], [-E0, H0], [0, E0]], channel_multiplier=1).then_inc(pool_step, 1)
            pool.wait_ge(pool_step, 4)
            nc.gpsimd.affine_select(out=hm, in_=hm, compare_op=ALU.is_ge, fill=0.0, base=E0 - 1,
                                    pattern=[[0, GB], [E0, H0], [0, E0]], channel_multiplier=-1).then_inc(pool_const, 1)
            POOL0 = 4
            pool.wait_ge(in_vw, 32)
            nc.gpsimd.tensor_copy(w_heads.rearrange("d (h v) -> d h v", h=H),
                                  w_raw.rearrange("d (v h) -> d h v", h=H)).then_inc(w_heads_ready, 1)

            def inv_std(n, j, w, phase=None):
                pool.wait_ge(mv_ready, count(n + 1))
                if above_0(n - 1):
                    pool.wait_ge(xn_ready, count(n - 1))
                if w == GT and above_0(act_no(phase, n) - 1):
                    pool.wait_ge(xn_act_ready, count(act_no(phase, n) - 1))
                if w == GT:
                    nc.gpsimd.tensor_tensor(neg_mean[:, j, :], mv[:, j, :, 0], minus_1[:], ALU.mult).then_inc(neg_mean_ready, 1)
                nc.gpsimd.tensor_tensor(veps[:, j, 0:w], mv[:, j, 0:w, 1], eps_t[:, 0:w], ALU.add).then_inc(pool_step, 1)
                pool.wait_ge(pool_step, count(n + (POOL0 + 1)))
                nc.gpsimd.tensor_tensor(rstd[:, j, 0:w], veps[:, j, 0:w], half_neg[:, 0:w], ALU.pow).then_inc(rstd_ready, 1)
                if w == GT:
                    pool.wait_ge(rstd_ready, count(n + 1))
                    pool.wait_ge(neg_mean_ready, count(act_no(phase, n) + 1))
                    nc.gpsimd.tensor_tensor(shift[:, j, :], neg_mean[:, j, :], rstd[:, j, :], ALU.mult).then_inc(shift_ready, 1)

            def g_inv_std(phase):
                return lambda g, j: inv_std(ln_no(phase, g), j, GT, phase)

            phases(pool, [[(2 if phase == LIN else 3, g_inv_std(phase))] for phase in (FFN1, LIN, FFN2, SPEC1)])

            def scale_probs(n, j):
                pool.wait_ge(rinv_ready, count(n + 1))
                r = rinv[:, j, :].rearrange("p (h q) -> p h q", h=2)
                nc.gpsimd.tensor_tensor(pr[:, j, :, 0, :], pr[:, j, :, 0, :],
                                        r[:, :, 0:1].to_broadcast([P, 2, P]), ALU.mult)
                nc.gpsimd.tensor_tensor(pr[:, j, :, 1:3, :].rearrange("p h b k -> p h (b k)"),
                                        pr[:, j, :, 1:3, :].rearrange("p h b k -> p h (b k)"),
                                        r[:, :, 1:2].to_broadcast([P, 2, 2 * P]), ALU.mult).then_inc(pn_ready, 1)

            inv_std(LN_SOFT, 0, BT)

            def batch(b, jb, first=False, last=False):
                for p in range(PAIRS):
                    scale_probs(b * PAIRS + p, p % 2)
                    if p == 1 and not last:
                        inv_std(b + (LN_SOFT + 1), 1 - jb, BT)

            batches(pool, batch)
            phases(pool, [[(3, g_inv_std(SPEC2))]])

        @block.vector
        def _(dve):
            nc.vector.memset(bias_bf[:], 0.0)
            nc.vector.memset(biasq_bf[:], 0.0)
            nc.vector.memset(kvrow[:], 0.0)
            dve.wait_ge(in_small, 16 * SMALL_LOADS)
            row = [0]

            def rowstep(ins):
                row[0] += 1
                ins.then_inc(su_row, 1)
                dve.wait_ge(su_row, count(row[0]))

            def rep(dst, at, n, times):
                src = rows[0:1, at:at + n].unsqueeze(1).to_broadcast([1, times, n])
                return nc.vector.tensor_copy(dst.rearrange("p (a n) -> p a n", a=times), src)

            rowstep(rep(bwide[:, FFN_B, :], BFFN, D, 4))
            rowstep(rep(bwide[:, FFT_B, :], BFFT, D, 4))
            rowstep(nc.vector.tensor_scalar(bwide[:, FFT_B, :], bwide[:, FFT_B, :], 0.5, None, ALU.mult))
            rowstep(rep(bwide[:, BO_B, :], BO, D, 4))
            dve.wait_ge(su_pe, 3)
            bu_kv = rows[0:1, BU:BU + 2 * D].rearrange("p (h s e) -> p s h e", s=2, e=E0)
            for s in range(2):
                rowstep(nc.vector.tensor_tensor(kvrow[:, s * D:(s + 1) * D].rearrange("p (h e) -> p h e", e=E0),
                                                ps[0:1, 4, s * D:(s + 1) * D].rearrange("p (h e) -> p h e", e=E0),
                                                bu_kv[:, s], ALU.add))
            rowstep(nc.vector.tensor_scalar(kvrow[:, 0:D], kvrow[:, 0:D], 1.0, None, ALU.add))
            rowstep(nc.vector.tensor_copy(bwide[:, KV_B, :].rearrange("p (a n) -> p a n", a=2),
                                          kvrow[:].unsqueeze(1).to_broadcast([1, 2, 2 * D])))
            rowstep(nc.vector.tensor_scalar(bwide[:, 4, 0:D], rows[:, BQ:BQ + D], 1.0, None, ALU.add))
            for i in range(5):
                n = 512 if i < 4 else D
                dst = bias_bf[:, i, :] if i < 4 else biasq_bf[:]
                cur = bwide[:, i, 0:n]
                for part in range(3):
                    piece = dst[32 * part:32 * part + 1, 0:n]
                    rowstep(nc.vector.tensor_copy(piece, cur))
                    if part < 2:
                        nxt = rest[:, part, 0:n]
                        rowstep(nc.vector.tensor_copy(nxt, piece))
                        rowstep(nc.vector.tensor_tensor(nxt, cur, nxt, ALU.subtract))
                        cur = nxt
            nc.vector.memset(kvrow[:, 0:1], 0.0).then_inc(su_x, 1)

            def big_lo():
                for i in range(4):
                    dve.wait_ge(su_hi, count(i + 1))
                    nc.vector.scalar_tensor_tensor(out=g_lo[:, 4 * i:4 * i + 4, :].rearrange("p h d -> p (h d)"),
                                                   in0=ps[:, i % 4, :], scalar=SCORE_SCALE,
                                                   in1=g_hi[:, 4 * i:4 * i + 4, :].rearrange("p h d -> p (h d)").bitcast(F32),
                                                   op0=ALU.mult, op1=ALU.subtract).then_inc(su_lo, 1)
                for i in range(2):
                    dve.wait_ge(su_hi, count(4 + i + 1))
                    nc.vector.tensor_tensor(v_lo[:, 512 * i:512 * i + 512], ps[:, 4 + i, :],
                                            v_hi[:, 512 * i:512 * i + 512].bitcast(F32), ALU.subtract).then_inc(su_lo, 1)
            big_lo()

            def stats(n, xs, w, j, x_at):
                if above_0(x_at):
                    dve.wait_ge(x_ready, count(x_at))
                for t in range(w):
                    last = nc.vector.bn_stats(bst[:, j, t, :], xs(t))
                last.then_inc(stats_done, 1)
                dve.wait_ge(stats_done, count(n + 1))
                nc.vector.memset(pause[:, 4:5], 0.0)
                for t in range(w):
                    last = nc.vector.bn_aggr(mv[:, j, t, :], bst[:, j, t, :])
                last.then_inc(mv_ready, 1)

            def normalise(n, xs, w, j):
                dve.wait_ge(rstd_ready, count(n + 1))
                if above_0(n - 1):
                    dve.wait_ge(tr_done, count(n - 1))
                for t in range(w):
                    last = nc.vector.tensor_scalar(xn[:, j, t * D:(t + 1) * D], xs(t), mv[:, j, t, 0:1],
                                                   rstd[:, j, t:t + 1], ALU.subtract, ALU.mult)
                last.then_inc(xn_ready, 1)

            def g_stats(phase):
                return lambda g, j: stats(ln_no(phase, g), lambda t: xg(g, t, 1), GT, j,
                                          {FFN1: 0, SPEC2: X_BEFORE[SPEC2]}.get(phase, g + ((phase - 1) * G + 1)))

            def g_norm(phase):
                return lambda g, j: normalise(ln_no(phase, g), lambda t: xg(g, t, 1), GT - ACT_TILES, j)

            dve.wait_ge(in_first, 16)
            dve.wait_ge(in_rest, 16)

            def add_tanh(k):
                def f(g, j):
                    dve.wait_ge(th_ready, count(g + (k * G + 1)))
                    nc.vector.scalar_tensor_tensor(out=xg(g), in0=th[:, j, :], scalar=0.5, in1=xg(g),
                                                   op0=ALU.mult, op1=ALU.add).then_inc(x_ready, 1)
                return f

            def add_bank(done, base, bank):
                def f(g, j):
                    dve.wait_ge(done, count(g + (base + 1)))
                    nc.vector.tensor_tensor(xg(g), ps[:, bank(j), :], xg(g), ALU.add).then_inc(x_ready, 1)
                return f

            def phi_k(g, j):
                dve.wait_ge(v0_ready, count(g + 1))
                if above_0(g):
                    dve.wait_ge(ctx_done, count(g))
                nc.vector.scalar_tensor_tensor(out=phk[:], in0=ek[:], scalar=1.0, in1=kv[:, :, 0:P],
                                               op0=ALU.min, op1=ALU.max).then_inc(phi_ready, 1)

            def phi_q(g, j):
                dve.wait_ge(eq_ready, count(g + 1))
                if above_0(g - 1):
                    dve.wait_ge(nd_done, count(g - 1))
                nc.vector.scalar_tensor_tensor(out=phq[:, j, :], in0=eq[:], scalar=1.0, in1=ps[:, LIN_Q, :],
                                               op0=ALU.min, op1=ALU.max).then_inc(phi_ready, 1)

            def context_mask(g, j):
                dve.wait_ge(ctx_done, count(g + 1))
                if above_0(g):
                    dve.wait_ge(nd_done, count(g))
                c = ps[:, LIN_C, :].rearrange("p (b n) -> p b n", b=GB)
                nc.vector.tensor_tensor(cbd[:, :, 0:P], c[:, :, 0:P], head_mask[:], ALU.mult)
                nc.vector.tensor_tensor(cbd[:, :, P:], head_mask[:].rearrange("p b (h e) -> p b h e", e=E0)[:, :, :, 0],
                                        c[:, :, P:P + 1].to_broadcast([P, GB, H0]), ALU.mult).then_inc(cbd_ready, 1)

            def z_and_y(g, j):
                dve.wait_ge(nd_done, count(g + 1))
                nc.vector.tensor_scalar(den[:], num_den[:, :, P:P + H0], Z_EPS, None, ALU.add).then_inc(den_ready, 1)
                dve.wait_ge(den_ready, count(g + 1))
                nc.vector.reciprocal(zr[:], den[:]).then_inc(zr_ready, 1)
                dve.wait_ge(zr_ready, count(g + 1))
                if above_0(g):
                    dve.wait_ge(y0t_done, count(g))
                nc.vector.tensor_tensor(y0[:].rearrange("p t (h e) -> p t h e", e=E0),
                                        num_den[:, :, 0:P].rearrange("p t (h e) -> p t h e", e=E0),
                                        zr[:].unsqueeze(3).to_broadcast([P, GT, H0, E0]), ALU.mult).then_inc(y0_ready, 1)

            phases(dve, [[(4, g_stats(FFN1)), (3, g_norm(FFN1)), (0, add_tanh(0))],
                         [(2, g_norm(LIN)), (0, z_and_y), (3, g_stats(LIN)), (1, phi_k), (1, phi_q),
                          (0, add_bank(mm_done, G, lambda j: LIN_O)), (1, context_mask)],
                         [(4, g_stats(FFN2)), (3, g_norm(FFN2)), (0, add_tanh(1))],
                         [(0, add_bank(mm_done, 3 * G, lambda j: BANK_OUT + j)), (4, g_stats(SPEC1)), (3, g_norm(SPEC1))]])

            def ln_soft_stats(b, j):
                stats(b + LN_SOFT, lambda t: xb(b, t, 1), BT, j, 4 * G)

            def ln_soft_norm(b, j):
                normalise(b + LN_SOFT, lambda t: xb(b, t, 1), BT, j)

            def x_low(b, j):
                dve.wait_ge(xhi_ready, count(b + 1))
                nc.vector.tensor_tensor(x_lo[:, j, :], ps[:, BANK_X, 0:T], x_hi[:, j, :].bitcast(F32), ALU.subtract).then_inc(xlo_ready, 1)

            def u_low(n, j):
                dve.wait_ge(uhi_ready, count(n + 1))
                if above_0(2 * n - 2):
                    dve.wait_ge(s_done, count(2 * n - 2))
                nc.vector.tensor_tensor(u_lo[:, j].rearrange("p h k -> p (h k)"), ps[:, BANK_U, :],
                                        u_hi[:, j].rearrange("p h k -> p (h k)").bitcast(F32), ALU.subtract).then_inc(ulo_ready, 1)

            def mask_scores(n, j):
                dve.wait_ge(s_done, count(2 * n + 1))
                if above_0(2 * n - 2):
                    dve.wait_ge(exp_ready, count(2 * n - 2))
                for qt in range(2):
                    w = (qt + 1) * P
                    if qt == 1:
                        dve.wait_ge(s_done, count(2 * n + 2))
                    nc.vector.memset(pause[:, 2 * j + qt:2 * j + qt + 1], 0.0)
                    for h in range(2):
                        o = ps[:, BANK_S + 2 * j + qt, h * w:(h + 1) * w]
                        last = nc.vector.tensor_tensor_reduce(o, o, mask[:, T - w:T], -1.0, -MASKED, ALU.add, ALU.min,
                                                              neg_max[:, j, 2 * h + qt:2 * h + qt + 1])
                    last.then_inc(max_ready, 1)

            def inv_sum(n, j):
                dve.wait_ge(exp_ready, count(2 * n + 2))
                if above_0(n - 1):
                    dve.wait_ge(pn_ready, count(n - 1))
                nc.vector.reciprocal(rinv[:, j, :], rsum[:, j, :]).then_inc(rinv_ready, 1)

            def probs_T(n, j):
                dve.wait_ge(pt_done, count(n + 1))
                if above_0(n - 1):
                    dve.wait_ge(pv_done, count(n - 1))
                nc.vector.tensor_copy(pT[:, j].rearrange("p h b q -> p (h b q)")[:, 0:512],
                                      ps[:, BANK_T, :]).then_inc(pTa_ready, 1)

            def add_z(b, j):
                dve.wait_ge(w_done, count(b + 1))
                nc.vector.tensor_tensor(xb(b), ps[:, BANK_X, 0:BT * D], xb(b), ALU.add).then_inc(x_ready, 1)

            ln_soft_stats(0, 0)
            ln_soft_norm(0, 0)
            x_low(0, 0)
            u_low(0, 0)
            u_low(1, 1)
            mask_scores(0, 0)
            u_low(2, 0)
            mask_scores(1, 1)

            def batch(b, jb, first=False, last=False):
                for p in range(PAIRS):
                    n, j = b * PAIRS + p, p % 2
                    inv_sum(n, j)
                    if not (first and p == 0):
                        probs_T(n - 1, 1 - j)
                    if not (last and p >= PAIRS - 3):
                        u_low(n + 3, 1 - j)
                    if not (last and p >= PAIRS - 2):
                        mask_scores(n + 2, j)
                    if p == 0 and not last:
                        ln_soft_stats(b + 1, 1 - jb)
                    if p == 1 and not first:
                        add_z(b - 1, 1 - jb)
                    if p == 1 and not last:
                        ln_soft_norm(b + 1, 1 - jb)
                    if p == 2 and not last:
                        x_low(b + 1, 1 - jb)

            batches(dve, batch)
            probs_T(B * PAIRS - 1, 1)
            add_z(B - 1, 1)
            phases(dve, [[(0, add_bank(mm_done, 4 * G, lambda j: BANK_OUT + j)), (4, g_stats(SPEC2)), (3, g_norm(SPEC2))]])

        @block.scalar
        def _(act):
            for dst, src in ((w123_s[:, 0, :], W1), (w123_s[:, 1, :], W2), (w123_s[:, 2, :], W3), (wd_s[:], Wd),
                             (wu_s[:], Wu), (wre_s[:], w_re), (wim_s[:], w_im),
                             (dft_s[:].rearrange("p a d -> p (a d)"), dft), (wq_s[:], Wq), (wo_s[:], Wo),
                             (bd_s[:], bd.unsqueeze(1)), (rows[:, BQ:BQ + D], bq.unsqueeze(0)),
                             (rows[:, BFFN:BFFN + D], ffn_bias.unsqueeze(0)), (rows[:, BFFT:BFFT + D], fft_bias.unsqueeze(0)),
                             (rows[:, BO:BO + D], bo.unsqueeze(0)), (rows[:, BU:BU + 2 * D], bu.unsqueeze(0))):
                act.dma_start(dst, src).then_inc(in_small, 16)
            act.wait_ge(su_pe, 1)
            nc.scalar.copy(wt_s[:, 0:2, :].rearrange("p a d -> p (a d)"), ps[:, 0, 0:2 * D])
            nc.scalar.copy(wt_s[0:R, 2, :], ps[0:R, 0, 2 * D:3 * D]).then_inc(su_ev, 1)
            act.wait_ge(su_pe, 2)
            nc.scalar.copy(abT[:, 0, :], ps[:, 1, 0:D])
            nc.scalar.mul(abT[:, 1, :], ps[:, 2, 0:D], -1.0).then_inc(su_ev, 1)
            act.wait_ge(su_pe, 3)
            nc.scalar.copy(w23[:], ps[:, 3, 0:D])
            nc.scalar.copy(wkv[:], ps[:, 3, D:3 * D]).then_inc(su_ev, 1)
            act.wait_ge(su_pe, 4)
            nc.scalar.copy(wc[:], ps[:, 5, 0:D])
            nc.scalar.mul(circ[:], ps[:, 6, 0:D], 0.5 / D).then_inc(su_ev, 1)
            for i in range(4):
                act.wait_ge(su_pe, count(5 + i))
                nc.scalar.mul(g_hi[:, 4 * i:4 * i + 4, :].rearrange("p h d -> p (h d)"), ps[:, i, :], SCORE_SCALE).then_inc(su_hi, 1)
            for i in range(2):
                act.wait_ge(su_pe, count(9 + i))
                nc.scalar.copy(v_hi[:, 512 * i:512 * i + 512], ps[:, 4 + i, :]).then_inc(su_hi, 1)
            for i in range(2):
                act.wait_ge(su_pe, count(11 + i))
                nc.scalar.mul(wz[:, 4 * i:4 * i + 4, :].rearrange("p h d -> p (h d)"), ps[:, 6 + i, :], OUT_SCALE).then_inc(su_ev, 1)

            def act_norm(phase):
                def f(g, j):
                    n = ln_no(phase, g)
                    act.wait_ge(shift_ready, count(act_no(phase, n) + 1))
                    if above_0(n - 1):
                        act.wait_ge(tr_done, count(n - 1))
                    nc.scalar.copy(act_pause[:, j:j + 1], shift[:, j, 0:1])
                    for t in range(GT - ACT_TILES, GT):
                        last = nc.scalar.activation(xn[:, j, t * D:(t + 1) * D], xg(g, t, 1), ACT.Identity,
                                                    bias=shift[:, j, t:t + 1], scale=rstd[:, j, t:t + 1])
                    last.then_inc(xn_act_ready, 1)
                return f

            def xT_out(phase):
                def f(g, j):
                    act.wait_ge(tr_done, count(ln_no(phase, g) + 1))
                    if phase == LIN and (isinstance(g, Count) or g >= 2):
                        act.wait_ge(q_done, count(g - 1))
                        act.wait_ge(kv_done, count(g - 1))
                    else:
                        if above_0(g + (phase * G - 1)):
                            act.wait_ge(mm_done, count(g + (phase * G - 1)))
                    nc.scalar.copy(xT[:, j, :], ps[:, 0 if phase == LIN else j, :]).then_inc(xT_ready, 1)
                return f

            def tanh(phase, k):
                def f(g, j):
                    act.wait_ge(mm_done, count(g + (phase * G + 1)))
                    if above_0(g + (phase * G - 1)):
                        act.wait_ge(x_ready, count(g + (phase * G - 1)))
                    nc.scalar.activation(th[:, j, :], ps[:, BANK_OUT + j, :], ACT.Tanh).then_inc(th_ready, 1)
                return f

            def exp_k(g, j):
                act.wait_ge(kv_done, count(g + 1))
                if above_0(2 * g - 1):
                    act.wait_ge(phi_ready, count(2 * g - 1))
                nc.scalar.activation(ek[:], kv[:, :, 0:P], ACT.Exp, bias=-1.0).then_inc(ek_ready, 1)

            def values_lin(g, j):
                if above_0(g):
                    act.wait_ge(ctx_done, count(g))
                nc.scalar.copy(vones[:, :, 0:P], kv[:, :, P:2 * P]).then_inc(v0_ready, 1)

            def exp_q(g, j):
                act.wait_ge(q_done, count(g + 1))
                if above_0(2 * g):
                    act.wait_ge(phi_ready, count(2 * g))
                nc.scalar.activation(eq[:], ps[:, LIN_Q, :], ACT.Exp, bias=-1.0).then_inc(eq_ready, 1)

            def y0T_out(g, j):
                act.wait_ge(y0t_done, count(g + 1))
                act.wait_ge(mm_done, count(g + G))
                nc.scalar.copy(yT0[:], ps[:, LIN_C, :]).then_inc(yT0_ready, 1)

            phases(act, [[(2, xT_out(FFN1)), (3, act_norm(FFN1)), (1, tanh(FFN1, 0))],
                         [(2, act_norm(LIN)), (1, exp_k), (0, y0T_out), (1, values_lin), (1, exp_q), (2, xT_out(LIN))],
                         [(2, xT_out(FFN2)), (3, act_norm(FFN2)), (1, tanh(FFN2, 1))],
                         [(2, xT_out(SPEC1)), (3, act_norm(SPEC1))]])

            def x_high(b, j):
                act.wait_ge(tr_done, count(b + (LN_SOFT + 1)))
                if above_0(2 * PAIRS * (b - 1)):
                    act.wait_ge(s_done, count(2 * PAIRS * (b - 1)))
                nc.scalar.copy(x_hi[:, j, :], ps[:, BANK_X, 0:T]).then_inc(xhi_ready, 1)

            def u_high(n, j):
                act.wait_ge(u_done, count(n + 1))
                if above_0(2 * n - 2):
                    act.wait_ge(s_done, count(2 * n - 2))
                nc.scalar.copy(u_hi[:, j].rearrange("p h k -> p (h k)"), ps[:, BANK_U, :]).then_inc(uhi_ready, 1)

            def exp_tile(n, j, qt):
                act.wait_ge(max_ready, count(2 * n + (1 + qt)))
                if qt == 0:
                    if above_0(n - 1):
                        act.wait_ge(pt_done, count(n - 1))
                    if above_0(n - 1):
                        act.wait_ge(rinv_ready, count(n - 1))
                w = (qt + 1) * P
                for h in range(2):
                    at = 2 * h + qt
                    dst = pr[:, j, h, 0, :] if qt == 0 else pr[:, j, h, 1:3, :].rearrange("p b k -> p (b k)")
                    last = nc.scalar.activation(dst, ps[:, BANK_S + 2 * j + qt, h * w:(h + 1) * w], ACT.Exp,
                                                bias=neg_max[:, j, at:at + 1], scale=-1.0, accum_out=rsum[:, j, at:at + 1])
                last.then_inc(exp_ready, 1)

            def probs_T(n, j):
                act.wait_ge(pt_done, count(n + 1))
                if above_0(n - 1):
                    act.wait_ge(pv_done, count(n - 1))
                nc.scalar.copy(pT[:, j].rearrange("p h b q -> p (h b q)")[:, 512:768], ps[:, BANK_T + 1, 0:256]).then_inc(pTb_ready, 1)

            def values_out(b, j, c):
                act.wait_ge(v_done, count(4 * b + (c + 1)))
                if c == 0:
                    if above_0(PAIRS * (b - 1)):
                        act.wait_ge(pv_done, count(PAIRS * (b - 1)))
                nc.scalar.copy(vv[:, j, c % 2, 512 * (c // 2):512 * (c // 2) + 512], ps[:, BANK_X, :]).then_inc(v_ready, 1)

            def y_out(b, jb, p):
                act.wait_ge(pv_done, count(b * PAIRS + (p + 1)))
                if p == 0:
                    if above_0(b - 1):
                        act.wait_ge(w_done, count(b - 1))
                nc.scalar.copy(yT[:, jb, p, :], y_bank).then_inc(y_ready, 1)

            x_high(0, 0)
            u_high(0, 0)
            u_high(1, 1)
            u_high(2, 0)
            exp_tile(0, 0, 0)
            exp_tile(0, 0, 1)
            for c in range(4):
                values_out(0, 0, c)

            def batch(b, jb, first=False, last=False):
                for p in range(PAIRS):
                    n, j = b * PAIRS + p, p % 2
                    if not (first and p == 0):
                        probs_T(n - 1, 1 - j)
                    if not (last and p >= PAIRS - 3):
                        u_high(n + 3, 1 - j)
                    if not (last and p >= PAIRS - 1):
                        exp_tile(n + 1, 1 - j, 0)
                    if p > 0:
                        y_out(b, jb, p - 1)
                    elif not first:
                        y_out(b - 1, 1 - jb, PAIRS - 1)
                    if not (last and p >= PAIRS - 1):
                        exp_tile(n + 1, 1 - j, 1)
                    if p == 2 and not last:
                        x_high(b + 1, 1 - jb)
                    if p >= V_TURN and not last:
                        values_out(b + 1, 1 - jb, p - V_TURN)

            batches(act, batch)
            probs_T(B * PAIRS - 1, 1)
            y_out(B - 1, 1, PAIRS - 1)
            phases(act, [[(2, xT_out(SPEC2)), (3, act_norm(SPEC2))]])

        @block.tensor
        def _(pe):
            mm, tr = nc.tensor.matmul, nc.tensor.transpose
            wu_kv = wu_s[:].rearrange("r (h s e) -> r s h e", s=2, e=E0)
            pe.wait_ge(pool_const, 3)
            pe.wait_ge(in_small, 16 * SMALL_LOADS)
            tr(ps[:, 0, 0:D], w123_s[:, 0, :], ident[:])
            tr(ps[:, 0, D:2 * D], w123_s[:, 1, :], ident[:])
            tr(ps[0:R, 0, 2 * D:3 * D], wd_s[:], ident[:]).then_inc(su_pe, 1)
            cos, sin, nsin = (dft_s[:, k, :] for k in range(3))
            mm(ps[:, 1, 0:D], wre_s[:], cos, start=True, stop=False, skip_group_check=True)
            mm(ps[:, 1, 0:D], wim_s[:], sin, start=False, stop=True, skip_group_check=True)
            mm(ps[:, 2, 0:D], wim_s[:], cos, start=True, stop=False, skip_group_check=True)
            mm(ps[:, 2, 0:D], wre_s[:], nsin, start=False, stop=True, skip_group_check=True).then_inc(su_pe, 1)
            pe.wait_ge(su_ev, 1)
            mm(ps[:, 3, 0:D], wt_s[:, 1, :], w123_s[:, 2, :], start=True, stop=True)
            for s in range(2):
                mm(ps[:, 3, (1 + s) * D:(2 + s) * D], wt_s[0:R, 2, :], wu_kv[:, s], start=True, stop=True)
            for s in range(2):
                last = mm(ps[0:1, 4, s * D:(s + 1) * D], bd_s[:], wu_kv[:, s], start=True, stop=True)
            last.then_inc(su_pe, 1)
            pe.wait_ge(su_ev, 3)
            mm(ps[:, 5, 0:D], wt_s[:, 0, :], w23[:], start=True, stop=True)
            mm(ps[:, 6, 0:D], abT[:, 0, :], cos, start=True, stop=False, skip_group_check=True)
            mm(ps[:, 6, 0:D], abT[:, 1, :], sin, start=False, stop=True, skip_group_check=True).then_inc(su_pe, 1)
            pe.wait_ge(in_qk, 32)
            q_h = q_raw.rearrange("q (d h) -> q h d", h=H)
            k_h = k_raw.rearrange("q (d h) -> q h d", h=H)
            for h in range(H):
                last = mm(ps[:, h // 4, (h % 4) * D:(h % 4 + 1) * D], k_h[:, h, :], q_h[:, h, :], start=True, stop=True)
                if h % 4 == 3:
                    last.then_inc(su_pe, 1)
            pe.wait_ge(in_vw, 32)
            pe.wait_ge(su_ev, 4)
            pe.wait_ge(su_row, 6)
            v_h = v_raw.rearrange("v (d h) -> v h d", h=H)
            for h in range(H):
                last = tr(ps[:, 4 + h // 8, (h % 8) * DV:(h % 8 + 1) * DV], v_h[:, h, :], ident[0:DV, 0:DV])
                if h % 8 == 7:
                    last.then_inc(su_pe, 1)
            pe.wait_ge(w_heads_ready, 1)
            for p in range(PAIRS):
                last = tr(ps[:, 6 + p // 4, (p % 4) * D:(p % 4 + 1) * D], w_heads[:, p * P:(p + 1) * P], ident[:])
                if p % 4 == 3:
                    last.then_inc(su_pe, 1)
            pe.wait_ge(su_lo, 6)
            pe.wait_ge(su_ev, 6)
            pe.wait_ge(su_x, 1)

            def transpose(phase):
                def f(g, j):
                    n = g + phase * G
                    pe.wait_ge(xn_ready, count(ln_no(phase, g) + 1))
                    pe.wait_ge(xn_act_ready, count(n + 1))
                    if phase == LIN or isinstance(g, int) and g == 0:
                        if above_0(n):
                            pe.wait_ge(xT_ready, count(n))
                    elif above_0(n - 1):
                        pe.wait_ge(xT_ready, count(n - 1))
                    if phase == FFN2 and isinstance(g, int) and g == 1:
                        pe.wait_ge(phi_ready, 2 * G)
                    for t in range(GT):
                        last = tr(ps[:, 0 if phase == LIN else j, t * P:(t + 1) * P], xn[:, j, t * D:(t + 1) * D], ident[:])
                    last.then_inc(tr_done, 1)
                return f

            def product(phase, w, bias, freed, before):
                def f(g, j):
                    pe.wait_ge(xT_ready, count(g + (phase * G + 1)))
                    if phase == FFN2 and isinstance(g, int) and g == 0:
                        pe.wait_ge(y0_ready, G)
                    if above_0(g + (before - 1)):
                        pe.wait_ge(freed, count(g + (before - 1)))
                    bank = ps[:, BANK_OUT + j, :]
                    mm(bank, ones_bf[:, 0:P], bias_bf[:, bias, :], start=True, stop=False, skip_group_check=True)
                    for t in range(GT):
                        last = mm(bank[:, t * D:(t + 1) * D], xT[:, j, t * P:(t + 1) * P], w, start=False, stop=True,
                                  skip_group_check=True)
                    last.then_inc(mm_done, 1)
                return f

            def keys_values(g, j):
                pe.wait_ge(xT_ready, count(g + (G + 1)))
                if above_0(g):
                    pe.wait_ge(v0_ready, count(g))
                    pe.wait_ge(phi_ready, count(2 * g - 1))
                for k in range(2):
                    bank = ps[:, LIN_KV + k, :]
                    mm(bank, ones_bf[:, 0:P], bias_bf[:, KV_B, :], start=True, stop=False, skip_group_check=True)
                    for t in range(2):
                        last = mm(bank[:, t * 2 * D:(t + 1) * 2 * D], xT[:, j, (2 * k + t) * P:(2 * k + t + 1) * P],
                                  wkv[:], start=False, stop=True, skip_group_check=True)
                last.then_inc(kv_done, 1)

            def queries(g, j):
                if above_0(2 * g):
                    pe.wait_ge(phi_ready, count(2 * g))
                mm(ps[:, LIN_Q, :], biasq_bf[:], ones_bf[:], start=True, stop=False, skip_group_check=True)
                mm(ps[:, LIN_Q, :], wq_s[:], xT[:, j, :], start=False, stop=True, skip_group_check=True).then_inc(q_done, 1)

            def lin_context(g, j):
                pe.wait_ge(phi_ready, count(2 * g + 1))
                if above_0(g):
                    pe.wait_ge(yT0_ready, count(g))
                for b in range(GB):
                    for t in range(BT):
                        last = mm(ps[:, LIN_C, b * 2 * P:b * 2 * P + P + 1], phk[:, b * BT + t, :], vones[:, b * BT + t, :],
                                  start=(t == 0), stop=(t == BT - 1))
                last.then_inc(ctx_done, 1)

            def lin_outputs(g, j):
                pe.wait_ge(cbd_ready, count(g + 1))
                pe.wait_ge(phi_ready, count(2 * g + 2))
                if isinstance(g, int) and g == 0:
                    pe.wait_ge(th_ready, G)
                if above_0(g):
                    pe.wait_ge(y0_ready, count(g))
                for t in range(GT):
                    last = mm(num_den[:, t, 0:P + H0], phq[:, j, t * P:(t + 1) * P], cbd[:, t // BT, :],
                              start=True, stop=True, skip_group_check=True)
                last.then_inc(nd_done, 1)

            def y0_transpose(g, j):
                pe.wait_ge(y0_ready, count(g + 1))
                for t in range(GT):
                    last = tr(ps[:, LIN_C, t * P:(t + 1) * P], y0[:, t, :], ident[:])
                last.then_inc(y0t_done, 1)

            def lin_project_out(g, j):
                pe.wait_ge(yT0_ready, count(g + 1))
                pe.wait_ge(x_ready, count(g + G))
                mm(ps[:, LIN_O, :], ones_bf[:, 0:P], bias_bf[:, BO_B, :], start=True, stop=False, skip_group_check=True)
                for t in range(GT):
                    last = mm(ps[:, LIN_O, t * D:(t + 1) * D], yT0[:, t * P:(t + 1) * P], wo_s[:], start=False, stop=True,
                              skip_group_check=True)
                last.then_inc(mm_done, 1)

            phases(pe, [[(2, transpose(FFN1)), (1, product(FFN1, wc[:], FFN_B, th_ready, 0))],
                        [(0, lin_outputs), (1, keys_values), (0, y0_transpose), (1, queries), (0, lin_project_out),
                         (1, lin_context), (2, transpose(LIN))],
                        [(2, transpose(FFN2)), (1, product(FFN2, wc[:], FFN_B, th_ready, G))],
                        [(2, transpose(SPEC1)), (1, product(SPEC1, circ[:], FFT_B, x_ready, 3 * G))]])

            def x_transpose(b, j):
                pe.wait_ge(xn_ready, count(b + (LN_SOFT + 1)))
                for t in range(BT):
                    last = tr(ps[:, BANK_X, t * P:(t + 1) * P], xn[:, j, t * D:(t + 1) * D], ident[:])
                last.then_inc(tr_done, 1)

            def u_product(n, h2, jb, j):
                for k in range(2):
                    h = 2 * h2 + k
                    o = ps[:, BANK_U, k * T:(k + 1) * T]
                    mm(o, g_hi[:, h, :], x_hi[:, jb, :], start=True, stop=False, skip_group_check=True)
                    mm(o, g_hi[:, h, :], x_lo[:, jb, :], start=False, stop=False, skip_group_check=True)
                    last = mm(o, g_lo[:, h, :], x_hi[:, jb, :], start=False, stop=True, skip_group_check=True)
                last.then_inc(u_done, 1)

            def scores(n, jb, j):
                pe.wait_ge(ulo_ready, count(n + 1))
                if above_0(2 * n - 3):
                    pe.wait_ge(exp_ready, count(2 * n - 3))
                o = ps[:, BANK_S + 2 * j, 0:2 * P].rearrange("p (h k) -> p h k", h=2)
                uh, ul = (a[:, j, :, 0:P] for a in (u_hi, u_lo))
                xh, xl = x_hi[:, jb, 0:P], x_lo[:, jb, 0:P]
                mm(o, xh, uh, start=True, stop=False, skip_group_check=True)
                mm(o, xh, ul, start=False, stop=False, skip_group_check=True)
                mm(o, xl, uh, start=False, stop=True, skip_group_check=True).then_inc(s_done, 1)
                if above_0(2 * n - 2):
                    pe.wait_ge(exp_ready, count(2 * n - 2))
                o = ps[:, BANK_S + 2 * j + 1, :].rearrange("p (h k) -> p h k", h=2)
                uh, ul = u_hi[:, j], u_lo[:, j]
                xh, xl = x_hi[:, jb, P:2 * P], x_lo[:, jb, P:2 * P]
                mm(o, xh, uh, start=True, stop=False, skip_group_check=True)
                mm(o, xh, ul, start=False, stop=False, skip_group_check=True)
                mm(o, xl, uh, start=False, stop=True, skip_group_check=True).then_inc(s_done, 1)

            def probs_transpose(n, j):
                pe.wait_ge(pn_ready, count(n + 1))
                if above_0(n):
                    pe.wait_ge(pTa_ready, count(n))
                for k in range(6):
                    if k == 4 and above_0(n):
                        pe.wait_ge(pTb_ready, count(n))
                        pe.wait_ge(y_ready, count(n))
                    last = tr(ps[:, BANK_T + k // 4, (k % 4) * P:(k % 4 + 1) * P], pr[:, j, k // 3, k % 3, :], ident[:])
                last.then_inc(pt_done, 1)

            def values(b, j, c):
                at = slice(512 * (c // 2), 512 * (c // 2) + 512)
                tok = slice((c % 2) * P, (c % 2 + 1) * P)
                mm(ps[:, BANK_X, :], x_hi[:, j, tok], v_hi[:, at], start=True, stop=False, skip_group_check=True)
                mm(ps[:, BANK_X, :], x_hi[:, j, tok], v_lo[:, at], start=False, stop=False, skip_group_check=True)
                mm(ps[:, BANK_X, :], x_lo[:, j, tok], v_hi[:, at], start=False, stop=True, skip_group_check=True).then_inc(v_done, 1)

            def products(n, p, jb, j):
                pe.wait_ge(pTa_ready, count(n + 1))
                pe.wait_ge(pTb_ready, count(n + 1))
                for kt in range(BT):
                    for k in range(2):
                        h = 2 * p + k
                        last = mm(y_bank[k * DV:(k + 1) * DV, kt * P:T], vv[:, jb, kt, h * DV:(h + 1) * DV],
                                  pT[:, j, k, 0:2, :] if kt == 0 else pT[:, j, k, 2, :], start=(kt == 0), stop=(kt == 1),
                                  skip_group_check=True)
                last.then_inc(pv_done, 1)

            def project_out(b, j):
                pe.wait_ge(y_ready, count(PAIRS * (b + 1)))
                for t in range(BT):
                    for p in range(PAIRS):
                        last = mm(ps[:, BANK_X, t * D:(t + 1) * D], yT[:, j, p, t * P:(t + 1) * P], wz[:, p, :],
                                  start=(p == 0), stop=(p == PAIRS - 1))
                last.then_inc(w_done, 1)

            pe.wait_ge(x_ready, 4 * G)
            x_transpose(0, 0)
            pe.wait_ge(xlo_ready, 1)
            u_product(0, 0, 0, 0)
            pe.wait_ge(ulo_ready, 1)
            u_product(1, 1, 0, 1)
            scores(0, 0, 0)
            pe.wait_ge(ulo_ready, 2)
            u_product(2, 2, 0, 0)
            scores(1, 0, 1)
            values(0, 0, 0)
            for c in range(1, 4):
                pe.wait_ge(v_ready, c)
                values(0, 0, c)

            def batch(b, jb, first=False, last=False):
                for p in range(PAIRS):
                    n, j = b * PAIRS + p, p % 2
                    if not (last and p >= PAIRS - 3):
                        pe.wait_ge(ulo_ready, count(n + 3))
                        u_product(n + 3, (p + 3) % PAIRS, jb if p + 3 < PAIRS else 1 - jb, 1 - j)
                    if not (last and p >= PAIRS - 2):
                        scores(n + 2, jb if p + 2 < PAIRS else 1 - jb, j)
                    if p > 0:
                        products(n - 1, p - 1, jb, 1 - j)
                    elif not first:
                        products(n - 1, PAIRS - 1, 1 - jb, 1 - j)
                    if p == 1 and not first:
                        pe.wait_ge(v_ready, count(4 * (b + 1)))
                        project_out(b - 1, 1 - jb)
                    if p == 2 and not last:
                        if first:
                            pe.wait_ge(v_ready, 4)
                        else:
                            pe.wait_ge(x_ready, count(b + X_SOFT))
                        x_transpose(b + 1, 1 - jb)
                    if p == V_TURN and not last:
                        pe.wait_ge(xlo_ready, count(b + 2))
                    if p > V_TURN and not last:
                        pe.wait_ge(v_ready, count(4 * (b + 1) + (p - V_TURN)))
                    if p >= V_TURN and not last:
                        values(b + 1, 1 - jb, p - V_TURN)
                    probs_transpose(n, j)

            batches(pe, batch)
            products(B * PAIRS - 1, PAIRS - 1, 1, 1)
            pe.wait_ge(x_ready, X_SOFT + B - 1)
            project_out(B - 1, 1)
            phases(pe, [[(2, transpose(SPEC2)), (1, product(SPEC2, circ[:], FFT_B, x_ready, X_BEFORE[SPEC2]))]])


_INS = ["L0_attn_x", "L0_attn_Wq", "L0_attn_bq", "L0_attn_Wd", "L0_attn_bd", "L0_attn_Wu", "L0_attn_bu",
        "L0_attn_Wo", "L0_attn_bo", "L0_ffn_weight", "L0_ffn_aux_weight1", "L0_ffn_aux_weight2", "L0_ffn_bias",
        "L1_attn_Q", "L1_attn_K", "L1_attn_V", "L1_attn_W", "L1_ffn_w_freq_real", "L1_ffn_w_freq_imag", "L1_ffn_bias"]


def dft_tables():
    a = 2 * np.pi / D * (np.arange(D)[:, None] * np.arange(D)[None, :] % D)
    return np.concatenate([np.cos(a), np.sin(a), -np.sin(a)], axis=1).astype(np.float32)


def kernel(**inputs):
    import concourse.bacc as bacc
    from concourse.bass_utils import run_bass_kernel_spmd

    nc = bacc.Bacc("TRN2", target_bir_lowering=False, num_devices=1)
    arrays, args = {}, []
    for name in _INS:
        a = np.ascontiguousarray(inputs[name])
        arrays[name] = a
        args.append(nc.dram_tensor(name, a.shape, mybir.dt.from_np(a.dtype), kind="ExternalInput").ap())
    arrays["dft"] = dft_tables()
    args.append(nc.dram_tensor("dft", (D, 3 * D), F32, kind="ExternalInput").ap())
    args.append(nc.dram_tensor("out", (B, T, D), F32, kind="ExternalOutput").ap())
    build(nc, *args)
    r = run_bass_kernel_spmd(nc, [arrays], core_ids=[0])
    return r.results[0]["out"]
```

```python
import concourse.bass as bass
import numpy as np
from concourse import mybir
from contextlib import ExitStack

F32 = mybir.dt.float32
F32R = mybir.dt.float32r
BF16 = mybir.dt.bfloat16
ALU = mybir.AluOpType
ACT = mybir.ActivationFunctionType
AX = mybir.AxisListType

B, T, D = 32, 256, 128
P = 128
TILES = B * T // P
BT = T // P
G = 16
GT = TILES // G
GB = B // G
GW = GT * D
H0, R = 16, 32
E0 = D // H0
H, DQ, DV = 16, 64, 64
PAIRS = H // 2
EPS = 1e-5
Z_EPS = 1e-6
MASKED = -3.0e38
SCORE_SCALE = 1.0 / D
OUT_SCALE = 1.0 / H
LEAD = 5


class Count:

    def __init__(self, i, step=1, base=0):
        self.i, self.step, self.base = i, step, base

    def __add__(self, n):
        return Count(self.i, self.step, self.base + n)

    __radd__ = __add__

    def __sub__(self, n):
        return self + -n

    def __mul__(self, n):
        return Count(self.i, self.step * n, self.base * n)

    __rmul__ = __mul__


def count(n):
    return n.i * n.step + n.base if isinstance(n, Count) else n


def phases(eng, plan, early={}):
    def turn(stages, t):
        for lead, f in stages:
            if 0 <= t + lead < G:
                f(t + lead, (t + lead) % 2)
    last = (G - LEAD) // 2
    before = []
    for stages in plan:
        for t in range(-LEAD, 2):
            if t < 0:
                turn(before, G + t)
            if t in early and not before:
                early[t]()
            turn(stages, t)
        with eng.Fori(1, last) as i:
            for j in range(2):
                for lead, f in stages:
                    f(Count(i, 2, j + lead), (j + lead) % 2)
        for t in range(2 * last, G - LEAD):
            turn(stages, t)
        before = stages
    for t in range(G - LEAD, G):
        turn(before, t)


def batches(eng, batch):
    batch(0, 0, first=True)
    batch(1, 1)
    with eng.Fori(1, B // 2 - 1) as i:
        for j in range(2):
            batch(Count(i, 2, j), j)
    batch(B - 2, 0)
    batch(B - 1, 1, last=True)


def above_0(n):
    return isinstance(n, Count) or n > 0


def build(nc, x, Wq, bq, Wd, bd, Wu, bu, Wo, bo, W1, W2, W3, ffn_bias, Q, K, V, W, w_re, w_im, fft_bias, dft, out):
    ctx = ExitStack()
    with ctx:
        def sb(name, shape, dt=F32):
            return ctx.enter_context(nc.sbuf_tensor(name, shape, dt))

        def sem(name):
            return ctx.enter_context(nc.semaphore(name))

        x_all = sb("x_all", [P, TILES * D])
        ident = sb("ident", [P, P])
        mask = sb("mask", [P, T])
        ones_bf = sb("ones_bf", [P, 512], BF16)
        head_mask = sb("head_mask", [P, GB, P])
        wq_s = sb("wq_s", [P, D]); wd_s = sb("wd_s", [P, R]); wu_s = sb("wu_s", [R, 2 * D])
        bd_s = sb("bd_s", [R, 1]); wo_s = sb("wo_s", [P, D])
        w123_s = sb("w123_s", [P, 3, D]); wre_s = sb("wre_s", [P, D]); wim_s = sb("wim_s", [P, D])
        dft_s = sb("dft_s", [P, 3, D])
        rows = sb("rows", [1, 6 * D])
        BQ, FFN_B, FFT_B, BO_B, KV_B = 0, D, 2 * D, 3 * D, 4 * D
        space = sb("space", [P, 2 * BT * H * DV + 2 * PAIRS * T])
        q_raw, k_raw, v_raw = (space[0:DQ, k * D * H:(k + 1) * D * H] for k in range(3))
        w_raw = space[:, 3 * D * H:3 * D * H + DV * H]
        w_heads = space[:, 3 * D * H + DV * H:3 * D * H + 2 * DV * H]
        wt_s = sb("wt_s", [P, 3, D])
        w23 = sb("w23", [P, D]); wc = sb("wc", [P, D])
        wkv = sb("wkv", [P, 2 * D])
        abT = sb("abT", [P, 2, D]); circ = sb("circ", [P, D])
        bias_bf = sb("bias_bf", [P, 6 * D], BF16)
        kvrow = sb("kvrow", [1, 2 * D])
        rest = sb("rest", [1, 2, 4 * D])
        g_hi = sb("g_hi", [P, H, D], F32R); g_lo = sb("g_lo", [P, H, D], F32R)
        v_hi = sb("v_hi", [P, H * DV], F32R); v_lo = sb("v_lo", [P, H * DV], F32R)
        wz = sb("wz", [P, PAIRS, D])
        half_neg = sb("half_neg", [P, GT]); eps_t = sb("eps_t", [P, GT])
        bst = sb("bst", [P, 2, GT, 6]); mv = sb("mv", [P, 2, GT, 2])
        veps = sb("veps", [P, 2, GT]); rstd = sb("rstd", [P, 2, GT]); minus_1 = sb("minus_1", [P, GT])
        neg_mean = sb("neg_mean", [P, 2, GT]); shift = sb("shift", [P, 2, GT])
        act_pause = sb("act_pause", [P, 2])
        pause = sb("pause", [P, 7])
        z_bst = sb("z_bst", [P, BT, 6]); z_mv = sb("z_mv", [P, BT, 2]); z_veps = sb("z_veps", [P, BT])
        z_rstd = sb("z_rstd", [P, BT]); z_xn = sb("z_xn", [P, BT * D]); z_xT = sb("z_xT", [P, T])
        xn = sb("xn", [P, 2, GW])
        xT = sb("xT", [P, 2, GW])
        th = sb("th", [P, 2, GW])
        eq = sb("eq", [P, GW]); ek = sb("ek", [P, GT, P])
        phq = sb("phq", [P, 2, GW]); phk = sb("phk", [P, GT, P])
        vones = sb("vones", [P, GT, P + 1])
        cbd = sb("cbd", [P, GB, P + H0])
        den = sb("den", [P, GT, H0]); zr = sb("zr", [P, GT, H0])
        y0 = sb("y0", [P, GT, P]); yT0 = sb("yT0", [P, GW])
        x_hi = sb("x_hi", [P, 2, T], F32R); x_lo = sb("x_lo", [P, 2, T], F32R)
        u_hi = sb("u_hi", [P, 2, 2, T], F32R); u_lo = sb("u_lo", [P, 2, 2, T], F32R)
        neg_max = sb("neg_max", [P, 2, 4]); rsum = sb("rsum", [P, 2, 4]); rinv = sb("rinv", [P, 2, 4])
        pr = sb("pr", [P, 2, 2, 3, P])
        pT = sb("pT", [P, 2, 2, 3, P])
        vv = space[:, 0:2 * BT * H * DV].rearrange("p (r t n) -> p r t n", r=2, t=BT)
        yT = space[:, 2 * BT * H * DV:].rearrange("p (r a t) -> p r a t", r=2, a=PAIRS)

        ps = ctx.enter_context(nc.psum_tensor("ps", [P, 8, 512], F32))

        in_x = [sem(f"in_x{k}") for k in range(3)]; in_ffn = sem("in_ffn")
        in_small = sem("in_small"); in_bias = sem("in_bias"); in_qk = sem("in_qk"); in_vw = sem("in_vw")
        pool_const = sem("pool_const");
        su_pe = sem("su_pe"); su_ev = sem("su_ev"); su_row = sem("su_row"); bias_ready = sem("bias_ready")
        su_hi = sem("su_hi"); su_lo = sem("su_lo"); w_heads_ready = sem("w_heads_ready")
        stats_done = sem("stats_done"); mv_ready = sem("mv_ready")
        pool_step = sem("pool_step"); rstd_ready = sem("rstd_ready")
        shift_ready = sem("shift_ready"); neg_mean_ready = sem("neg_mean_ready")
        xn_ready = sem("xn_ready"); xn_act_ready = sem("xn_act_ready"); tr_done = sem("tr_done"); xT_ready = sem("xT_ready")
        mm_done = sem("mm_done"); th_ready = sem("th_ready"); x_ready = sem("x_ready")
        q_done = sem("q_done"); kv_done = sem("kv_done"); ek_ready = sem("ek_ready"); eq_ready = sem("eq_ready"); v0_ready = sem("v0_ready"); phi_ready = sem("phi_ready")
        ctx_done = sem("ctx_done"); cbd_ready = sem("cbd_ready"); nd_done = sem("nd_done")
        den_ready = sem("den_ready"); zr_ready = sem("zr_ready"); y0_ready = sem("y0_ready"); y0t_done = sem("y0t_done"); yT0_ready = sem("yT0_ready")
        u_done = sem("u_done"); uhi_ready = sem("uhi_ready"); ulo_ready = sem("ulo_ready")
        s_done = sem("s_done"); max_ready = sem("max_ready"); exp_ready = sem("exp_ready")
        rinv_ready = sem("rinv_ready"); pn_ready = sem("pn_ready"); pt_done = sem("pt_done")
        pTa_ready = sem("pTa_ready"); pTb_ready = sem("pTb_ready")
        pv_done = sem("pv_done"); y_ready = sem("y_ready")
        v_done = sem("v_done"); v_ready = sem("v_ready"); w_done = sem("w_done")
        xhi_ready = sem("xhi_ready"); xlo_ready = sem("xlo_ready")
        z_stats_done = sem("z_stats_done"); z_mv_ready = sem("z_mv_ready"); z_veps_ready = sem("z_veps_ready")
        z_rstd_ready = sem("z_rstd_ready"); z_xn_ready = sem("z_xn_ready"); z_tr_done = sem("z_tr_done")
        z_xT_ready = sem("z_xT_ready"); out_ready = sem("out_ready"); out_done = sem("out_done")

        block = ctx.enter_context(nc.Block())
        FFN_LOADS, SMALL_LOADS, BIAS_LOADS = 3, 8, 5
        X_LOADS = (0, 2, 5, G)

        def xg(g, t=0, n=GT):
            return x_all[:, bass.ds(count(g * GW + t * D), n * D)]

        def xb(b, t=0, n=BT):
            return x_all[:, bass.ds(count(b * (BT * D) + t * D), n * D)]

        LIN_Q, LIN_KV, LIN_C, LIN_N, LIN_O = 1, 2, 4, 5, 7
        kv = ps[:, LIN_KV:LIN_KV + 2, :].rearrange("p b (t n) -> p (b t) n", n=2 * P)
        num_den = ps[:, LIN_N:LIN_N + 2, :].rearrange("p b (t n) -> p (b t) n", n=2 * P)
        BANK_OUT = 5
        V_BANKS, W_BANKS = (4, 7), (0, 6)
        BANK_U, BANK_S, BANK_X, BANK_T = 0, 1, 5, 6
        FIRST_V_BANKS = (BANK_X, BANK_T, BANK_T + 1, BANK_X)
        y_bank = ps[:, BANK_T + 1, 512 - T:512]

        FFN1, LIN, FFN2, SPEC1 = range(4)
        SOFT = 4 * G

        ACT_TILES = {FFN1: 2, LIN: 2, FFN2: 2, SPEC1: 2}

        V_TURN = 4

        @block.sync
        def _(sp):
            def tiles_of(a, b0, b1):
                return a[b0:b1].rearrange("b (t p) d -> p (b t) d", p=P)
            for k, w in enumerate((W1, W2, W3)):
                sp.dma_start(w123_s[:, k, :], w).then_inc(in_ffn, 16)
            for loaded, g0, g1 in zip(in_x, X_LOADS, X_LOADS[1:]):
                if g0 == X_LOADS[2]:
                    for dst, src in ((bd_s[:], bd.unsqueeze(1)), (wd_s[:], Wd), (wu_s[:], Wu), (wq_s[:], Wq), (wo_s[:], Wo),
                                     (wre_s[:], w_re), (wim_s[:], w_im), (dft_s[:].rearrange("p a d -> p (a d)"), dft)):
                        sp.dma_start(dst, src).then_inc(in_small, 16)
                sp.dma_start(x_all[:, g0 * GW:g1 * GW].rearrange("p (t d) -> p t d", d=D), tiles_of(x, g0 * GB, g1 * GB)).then_inc(loaded, 16)
            sp.dma_start(q_raw, Q.rearrange("q d h -> q (d h)")).then_inc(in_qk, 16)
            sp.dma_start(k_raw, K.rearrange("q d h -> q (d h)")).then_inc(in_qk, 16)
            sp.dma_start(v_raw, V.rearrange("q d h -> q (d h)")).then_inc(in_vw, 16)
            sp.dma_start(w_raw, W.rearrange("d v h -> d (v h)")).then_inc(in_vw, 16)
            with sp.Fori(0, G) as i:
                g = Count(i)
                sp.wait_ge(out_ready, count(GB * g + GB))
                sp.dma_start(out[bass.ds(count(g * GB), GB)].rearrange("b (t p) d -> p (b t) d", p=P),
                             xg(g).rearrange("p (t d) -> p t d", d=D)).then_inc(out_done, 16)
            sp.wait_ge(out_done, 16 * G)

        @block.gpsimd
        def _(pool):
            nc.gpsimd.memset(ident[:], 0.0).then_inc(pool_step, 1)
            nc.gpsimd.memset(mask[:], 0.0).then_inc(pool_step, 1)
            nc.gpsimd.memset(head_mask[:], 1.0).then_inc(pool_step, 1)
            nc.gpsimd.memset(half_neg[:], -0.5)
            nc.gpsimd.memset(eps_t[:], EPS)
            nc.gpsimd.memset(minus_1[:], -1.0)
            nc.gpsimd.memset(ones_bf[:], 1.0)
            nc.gpsimd.memset(vones[:], 1.0)
            pool.wait_ge(pool_step, 3)
            nc.gpsimd.affine_select(out=ident[:], in_=ident[:], compare_op=ALU.not_equal, fill=1.0, base=0,
                                    pattern=[[-1, P]], channel_multiplier=1).then_inc(pool_const, 1)
            nc.gpsimd.affine_select(out=mask[:], in_=mask[:], compare_op=ALU.is_ge, fill=MASKED, base=P,
                                    pattern=[[-1, T]], channel_multiplier=1).then_inc(pool_const, 1)
            hm = head_mask[:].rearrange("p a (h e) -> p (a h) e", e=E0)
            nc.gpsimd.affine_select(out=hm, in_=hm, compare_op=ALU.is_ge, fill=0.0, base=0,
                                    pattern=[[0, GB], [-E0, H0], [0, E0]], channel_multiplier=1).then_inc(pool_step, 1)
            pool.wait_ge(pool_step, 4)
            nc.gpsimd.affine_select(out=hm, in_=hm, compare_op=ALU.is_ge, fill=0.0, base=E0 - 1,
                                    pattern=[[0, GB], [E0, H0], [0, E0]], channel_multiplier=-1).then_inc(pool_const, 1)
            POOL0 = 4

            def inv_std(n, j, w):
                pool.wait_ge(mv_ready, count(n + 1))
                if above_0(n - 1):
                    pool.wait_ge(xn_ready, count(n - 1))
                if w == GT and above_0(n - 1):
                    pool.wait_ge(xn_act_ready, count(n - 1))
                if w == GT:
                    nc.gpsimd.tensor_tensor(neg_mean[:, j, :], mv[:, j, :, 0], minus_1[:], ALU.mult).then_inc(neg_mean_ready, 1)
                nc.gpsimd.tensor_tensor(veps[:, j, 0:w], mv[:, j, 0:w, 1], eps_t[:, 0:w], ALU.add).then_inc(pool_step, 1)
                pool.wait_ge(pool_step, count(n + (POOL0 + 1)))
                nc.gpsimd.tensor_tensor(rstd[:, j, 0:w], veps[:, j, 0:w], half_neg[:, 0:w], ALU.pow).then_inc(rstd_ready, 1)
                if w == GT:
                    pool.wait_ge(rstd_ready, count(n + 1))
                    pool.wait_ge(neg_mean_ready, count(n + 1))
                    nc.gpsimd.tensor_tensor(shift[:, j, :], neg_mean[:, j, :], rstd[:, j, :], ALU.mult).then_inc(shift_ready, 1)

            def g_inv_std(phase):
                return lambda g, j: inv_std(g + phase * G, j, GT)

            phases(pool, [[(5, g_inv_std(phase))] for phase in (FFN1, LIN, FFN2, SPEC1)])

            def scale_probs(n, j):
                pool.wait_ge(rinv_ready, count(n + 1))
                r = rinv[:, j, :].rearrange("p (h q) -> p h q", h=2)
                nc.gpsimd.tensor_tensor(pr[:, j, :, 0, :], pr[:, j, :, 0, :],
                                        r[:, :, 0:1].to_broadcast([P, 2, P]), ALU.mult)
                nc.gpsimd.tensor_tensor(pr[:, j, :, 1:3, :].rearrange("p h b k -> p h (b k)"),
                                        pr[:, j, :, 1:3, :].rearrange("p h b k -> p h (b k)"),
                                        r[:, :, 1:2].to_broadcast([P, 2, 2 * P]), ALU.mult).then_inc(pn_ready, 1)

            pool.wait_ge(in_vw, 32)
            nc.gpsimd.tensor_copy(w_heads.rearrange("d (h v) -> d h v", h=H),
                                  w_raw.rearrange("d (v h) -> d h v", h=H)).then_inc(w_heads_ready, 1)
            def z_inv_std(b):
                pool.wait_ge(z_mv_ready, count(b + 1))
                if above_0(b):
                    pool.wait_ge(z_xn_ready, count(b))
                nc.gpsimd.tensor_tensor(z_veps[:], z_mv[:, :, 1], eps_t[:, 0:BT], ALU.add).then_inc(z_veps_ready, 1)
                pool.wait_ge(z_veps_ready, count(b + 1))
                nc.gpsimd.tensor_tensor(z_rstd[:], z_veps[:], half_neg[:, 0:BT], ALU.pow).then_inc(z_rstd_ready, 1)

            inv_std(SOFT, 0, BT)

            def batch(b, jb, first=False, last=False):
                for p in range(PAIRS):
                    scale_probs(b * PAIRS + p, p % 2)
                    if p == 1 and not last:
                        inv_std(b + (SOFT + 1), 1 - jb, BT)
                    if p == 4 and not first:
                        z_inv_std(b - 1)

            batches(pool, batch)
            z_inv_std(B - 1)

        @block.vector
        def _(dve):
            nc.vector.memset(bias_bf[:], 0.0)
            nc.vector.memset(kvrow[:], 0.0)
            steps = [0]

            def rowstep(ins):
                steps[0] += 1
                ins.then_inc(su_row, 1)
                dve.wait_ge(su_row, count(steps[0]))

            def split(cur, at, n):
                for part in range(3):
                    piece = bias_bf[32 * part:32 * part + 1, at:at + n]
                    rowstep(nc.vector.tensor_copy(piece, cur))
                    if part < 2:
                        nxt = rest[:, part, 0:n]
                        rowstep(nc.vector.tensor_copy(nxt, piece))
                        rowstep(nc.vector.tensor_tensor(nxt, cur, nxt, ALU.subtract))
                        cur = nxt

            def bias_parts():
                dve.wait_ge(in_bias, 16 * BIAS_LOADS)
                nc.vector.tensor_scalar(rows[:, BQ:BQ + D], rows[:, BQ:BQ + D], 1.0, None, ALU.add)
                rowstep(nc.vector.tensor_scalar(rows[:, FFT_B:FFT_B + D], rows[:, FFT_B:FFT_B + D], 0.5, None, ALU.mult))
                split(rows[:, 0:4 * D], 0, 4 * D)
                nc.vector.memset(kvrow[:, 0:1], 0.0).then_inc(bias_ready, 1)

            def bias_of_keys_values():
                dve.wait_ge(su_pe, 5)
                bu_kv = rows[0:1, KV_B:KV_B + 2 * D].rearrange("p (h s e) -> p s h e", s=2, e=E0)
                for s in range(2):
                    rowstep(nc.vector.tensor_tensor(kvrow[:, s * D:(s + 1) * D].rearrange("p (h e) -> p h e", e=E0),
                                                    ps[0:1, 7, s * D:(s + 1) * D].rearrange("p (h e) -> p h e", e=E0),
                                                    bu_kv[:, s], ALU.add))
                rowstep(nc.vector.tensor_scalar(kvrow[:, 0:D], kvrow[:, 0:D], 1.0, None, ALU.add))
                split(kvrow[:], KV_B, 2 * D)
                nc.vector.memset(rest[:, 0, 0:1], 0.0).then_inc(bias_ready, 1)

            def stats(n, xs, w, j, x_at):
                if above_0(x_at):
                    dve.wait_ge(x_ready, count(x_at))
                for t in range(w):
                    last = nc.vector.bn_stats(bst[:, j, t, :], xs(t))
                last.then_inc(stats_done, 1)
                dve.wait_ge(stats_done, count(n + 1))
                nc.vector.memset(pause[:, 4:5], 0.0)
                for t in range(w):
                    last = nc.vector.bn_aggr(mv[:, j, t, :], bst[:, j, t, :])
                last.then_inc(mv_ready, 1)

            def normalise(n, xs, w, j):
                dve.wait_ge(rstd_ready, count(n + 1))
                if above_0(n - 1):
                    dve.wait_ge(tr_done, count(n - 1))
                for t in range(w):
                    last = nc.vector.tensor_scalar(xn[:, j, t * D:(t + 1) * D], xs(t), mv[:, j, t, 0:1],
                                                   rstd[:, j, t:t + 1], ALU.subtract, ALU.mult)
                last.then_inc(xn_ready, 1)

            def g_stats(phase):
                def f(g, j):
                    if phase == FFN1 and isinstance(g, int) and g in X_LOADS:
                        dve.wait_ge(in_x[X_LOADS.index(g)], 16)
                    stats(g + phase * G, lambda t: xg(g, t, 1), GT, j, 0 if phase == FFN1 else g + ((phase - 1) * G + 1))
                return f

            def g_norm(phase):
                return lambda g, j: normalise(g + phase * G, lambda t: xg(g, t, 1), GT - ACT_TILES[phase], j)

            def add_tanh(k):
                def f(g, j):
                    dve.wait_ge(th_ready, count(g + (k * G + 1)))
                    nc.vector.scalar_tensor_tensor(out=xg(g), in0=th[:, j, :], scalar=0.5, in1=xg(g),
                                                   op0=ALU.mult, op1=ALU.add).then_inc(x_ready, 1)
                return f

            def add_bank(done, base, bank):
                def f(g, j):
                    dve.wait_ge(done, count(g + (base + 1)))
                    nc.vector.tensor_tensor(xg(g), ps[:, bank(j), :], xg(g), ALU.add).then_inc(x_ready, 1)
                return f

            def phi_k(g, j):
                dve.wait_ge(v0_ready, count(g + 1))
                if above_0(g):
                    dve.wait_ge(ctx_done, count(g))
                nc.vector.scalar_tensor_tensor(out=phk[:], in0=ek[:], scalar=1.0, in1=kv[:, :, 0:P],
                                               op0=ALU.min, op1=ALU.max).then_inc(phi_ready, 1)

            def phi_q(g, j):
                dve.wait_ge(eq_ready, count(g + 1))
                if above_0(g - 1):
                    dve.wait_ge(nd_done, count(g - 1))
                nc.vector.scalar_tensor_tensor(out=phq[:, j, :], in0=eq[:], scalar=1.0, in1=ps[:, LIN_Q, :],
                                               op0=ALU.min, op1=ALU.max).then_inc(phi_ready, 1)

            def context_mask(g, j):
                dve.wait_ge(ctx_done, count(g + 1))
                if above_0(g):
                    dve.wait_ge(nd_done, count(g))
                c = ps[:, LIN_C, :].rearrange("p (b n) -> p b n", b=GB)
                nc.vector.tensor_tensor(cbd[:, :, 0:P], c[:, :, 0:P], head_mask[:], ALU.mult)
                nc.vector.tensor_tensor(cbd[:, :, P:], head_mask[:].rearrange("p b (h e) -> p b h e", e=E0)[:, :, :, 0],
                                        c[:, :, P:P + 1].to_broadcast([P, GB, H0]), ALU.mult).then_inc(cbd_ready, 1)

            def z_and_y(g, j):
                dve.wait_ge(nd_done, count(g + 1))
                nc.vector.tensor_scalar(den[:], num_den[:, :, P:P + H0], Z_EPS, None, ALU.add).then_inc(den_ready, 1)
                dve.wait_ge(den_ready, count(g + 1))
                nc.vector.reciprocal(zr[:], den[:]).then_inc(zr_ready, 1)
                dve.wait_ge(zr_ready, count(g + 1))
                if above_0(g):
                    dve.wait_ge(y0t_done, count(g))
                nc.vector.tensor_tensor(y0[:].rearrange("p t (h e) -> p t h e", e=E0),
                                        num_den[:, :, 0:P].rearrange("p t (h e) -> p t h e", e=E0),
                                        zr[:].unsqueeze(3).to_broadcast([P, GT, H0, E0]), ALU.mult).then_inc(y0_ready, 1)

            phases(dve, [[(3, g_norm(FFN1)), (5, g_stats(FFN1)), (0, add_tanh(0))],
                         [(3, g_norm(LIN)), (0, z_and_y), (5, g_stats(LIN)), (1, phi_k), (1, phi_q), (1, context_mask),
                          (0, add_bank(mm_done, G, lambda j: LIN_O))],
                         [(3, g_norm(FFN2)), (5, g_stats(FFN2)), (0, add_tanh(1))],
                         [(3, g_norm(SPEC1)), (5, g_stats(SPEC1)), (0, add_bank(mm_done, 3 * G, lambda j: BANK_OUT + j))]],
                   early={-2: bias_parts, 1: bias_of_keys_values})

            def ln_soft_stats(b, j):
                stats(b + SOFT, lambda t: xb(b, t, 1), BT, j, 4 * G)

            def ln_soft_norm(b, j):
                normalise(b + SOFT, lambda t: xb(b, t, 1), BT, j)

            def x_low(b, j):
                dve.wait_ge(xhi_ready, count(b + 1))
                nc.vector.tensor_tensor(x_lo[:, j, :], ps[:, BANK_X, 0:T], x_hi[:, j, :].bitcast(F32), ALU.subtract).then_inc(xlo_ready, 1)

            def u_low(n, j):
                dve.wait_ge(uhi_ready, count(n + 1))
                if above_0(2 * n - 2):
                    dve.wait_ge(s_done, count(2 * n - 2))
                nc.vector.tensor_tensor(u_lo[:, j].rearrange("p h k -> p (h k)"), ps[:, BANK_U, :],
                                        u_hi[:, j].rearrange("p h k -> p (h k)").bitcast(F32), ALU.subtract).then_inc(ulo_ready, 1)

            def mask_scores(n, j):
                dve.wait_ge(s_done, count(2 * n + 1))
                if above_0(2 * n - 2):
                    dve.wait_ge(exp_ready, count(2 * n - 2))
                for qt in range(2):
                    w = (qt + 1) * P
                    if qt == 1:
                        dve.wait_ge(s_done, count(2 * n + 2))
                    nc.vector.memset(pause[:, 2 * j + qt:2 * j + qt + 1], 0.0)
                    for h in range(2):
                        o = ps[:, BANK_S + 2 * j + qt, h * w:(h + 1) * w]
                        last = nc.vector.tensor_tensor_reduce(o, o, mask[:, T - w:T], -1.0, -MASKED, ALU.add, ALU.min,
                                                              neg_max[:, j, 2 * h + qt:2 * h + qt + 1])
                    last.then_inc(max_ready, 1)

            def inv_sum(n, j):
                dve.wait_ge(exp_ready, count(2 * n + 2))
                if above_0(n - 1):
                    dve.wait_ge(pn_ready, count(n - 1))
                nc.vector.reciprocal(rinv[:, j, :], rsum[:, j, :]).then_inc(rinv_ready, 1)

            def probs_T(n, j):
                dve.wait_ge(pt_done, count(n + 1))
                if above_0(n - 1):
                    dve.wait_ge(pv_done, count(n - 1))
                nc.vector.tensor_copy(pT[:, j].rearrange("p h b q -> p (h b q)")[:, 0:512],
                                      ps[:, BANK_T, :]).then_inc(pTa_ready, 1)

            def add_z(b):
                dve.wait_ge(w_done, count(b + 1))
                nc.vector.tensor_tensor(xb(b), ps[:, BANK_X, 0:BT * D], xb(b), ALU.add).then_inc(x_ready, 1)

            def add_spectral(b, w_after):
                dve.wait_ge(w_done, count(w_after))
                nc.vector.tensor_tensor(xb(b), ps[:, BANK_X, BT * D:], xb(b), ALU.add).then_inc(out_ready, 1)

            def z_stats(b):
                dve.wait_ge(x_ready, count(b + (SOFT + 1)))
                nc.vector.memset(pause[:, 6:7], 0.0)
                for t in range(BT):
                    last = nc.vector.bn_stats(z_bst[:, t, :], xb(b, t, 1))
                last.then_inc(z_stats_done, 1)
                dve.wait_ge(z_stats_done, count(b + 1))
                nc.vector.memset(pause[:, 5:6], 0.0)
                for t in range(BT):
                    last = nc.vector.bn_aggr(z_mv[:, t, :], z_bst[:, t, :])
                last.then_inc(z_mv_ready, 1)

            def z_norm(b):
                dve.wait_ge(z_rstd_ready, count(b + 1))
                if above_0(b):
                    dve.wait_ge(z_tr_done, count(b))
                for t in range(BT):
                    last = nc.vector.tensor_scalar(z_xn[:, t * D:(t + 1) * D], xb(b, t, 1), z_mv[:, t, 0:1],
                                                   z_rstd[:, t:t + 1], ALU.subtract, ALU.mult)
                last.then_inc(z_xn_ready, 1)

            def g_low():
                for i in range(4):
                    dve.wait_ge(su_hi, count(i + 1))
                    nc.vector.scalar_tensor_tensor(out=g_lo[:, 4 * i:4 * i + 4, :].rearrange("p h d -> p (h d)"),
                                                   in0=ps[:, i % 4, :], scalar=SCORE_SCALE,
                                                   in1=g_hi[:, 4 * i:4 * i + 4, :].rearrange("p h d -> p (h d)").bitcast(F32),
                                                   op0=ALU.mult, op1=ALU.subtract).then_inc(su_lo, 1)

            def v_low():
                for i in range(2):
                    dve.wait_ge(su_hi, count(4 + i + 1))
                    nc.vector.tensor_tensor(v_lo[:, 512 * i:512 * i + 512], ps[:, V_BANKS[i], :],
                                            v_hi[:, 512 * i:512 * i + 512].bitcast(F32), ALU.subtract).then_inc(su_lo, 1)

            ln_soft_stats(0, 0)
            ln_soft_norm(0, 0)
            g_low()
            x_low(0, 0)
            v_low()
            u_low(0, 0)
            u_low(1, 1)
            mask_scores(0, 0)
            u_low(2, 0)
            mask_scores(1, 1)

            def batch(b, jb, first=False, last=False):
                for p in range(PAIRS):
                    n, j = b * PAIRS + p, p % 2
                    inv_sum(n, j)
                    if not (first and p == 0):
                        probs_T(n - 1, 1 - j)
                    if not (last and p >= PAIRS - 3):
                        u_low(n + 3, 1 - j)
                    if not (last and p >= PAIRS - 2):
                        mask_scores(n + 2, j)
                    if p == 0 and not last:
                        ln_soft_stats(b + 1, 1 - jb)
                    if p == 1 and not first:
                        add_z(b - 1)
                        if above_0(b - 1):
                            add_spectral(b - 2, b)
                    if p == 1 and not last:
                        ln_soft_norm(b + 1, 1 - jb)
                    if p == 3 and not last:
                        x_low(b + 1, 1 - jb)
                    if p == 3 and not first:
                        z_stats(b - 1)
                    if p == 6 and not first:
                        z_norm(b - 1)

            batches(dve, batch)
            probs_T(B * PAIRS - 1, 1)
            add_z(B - 1)
            add_spectral(B - 2, B)
            z_stats(B - 1)
            z_norm(B - 1)
            add_spectral(B - 1, B + 1)

        @block.scalar
        def _(act):
            for done, dst, src in ((in_bias, rows[:, FFN_B:FFN_B + D], ffn_bias.unsqueeze(0)), (in_bias, rows[:, BQ:BQ + D], bq.unsqueeze(0)),
                                   (in_bias, rows[:, FFT_B:FFT_B + D], fft_bias.unsqueeze(0)),
                                   (in_bias, rows[:, BO_B:BO_B + D], bo.unsqueeze(0)), (in_bias, rows[:, KV_B:KV_B + 2 * D], bu.unsqueeze(0))):
                act.dma_start(dst, src).then_inc(done, 16)
            act.wait_ge(su_pe, 1)
            nc.scalar.copy(wt_s[:, 0:2, :].rearrange("p a d -> p (a d)"), ps[:, 0, 0:2 * D]).then_inc(su_ev, 1)
            act.wait_ge(su_pe, 2)
            nc.scalar.copy(w23[:], ps[:, 2, 0:D]).then_inc(su_ev, 1)
            act.wait_ge(su_pe, 3)
            nc.scalar.copy(wc[:], ps[:, 3, 0:D]).then_inc(su_ev, 1)

            def small_out():
                act.wait_ge(su_pe, 4)
                nc.scalar.copy(wt_s[0:R, 2, :], ps[0:R, 2, 0:D])
                nc.scalar.copy(abT[:, 0, :], ps[:, 3, 0:D])
                nc.scalar.mul(abT[:, 1, :], ps[:, 3, D:2 * D], -1.0).then_inc(su_ev, 1)
                act.wait_ge(su_pe, 5)
                nc.scalar.copy(wkv[:], ps[:, 4, 0:2 * D])
                nc.scalar.mul(circ[:], ps[:, 2, D:2 * D], 0.5 / D).then_inc(su_ev, 1)

            def g_high():
                for i in range(4):
                    act.wait_ge(su_pe, count(6 + i))
                    nc.scalar.mul(g_hi[:, 4 * i:4 * i + 4, :].rearrange("p h d -> p (h d)"), ps[:, i, :], SCORE_SCALE).then_inc(su_hi, 1)

            def v_high():
                for i in range(2):
                    act.wait_ge(su_pe, count(10 + i))
                    nc.scalar.copy(v_hi[:, 512 * i:512 * i + 512], ps[:, V_BANKS[i], :]).then_inc(su_hi, 1)

            def w_out():
                for i in range(2):
                    act.wait_ge(su_pe, count(12 + i))
                    nc.scalar.mul(wz[:, 4 * i:4 * i + 4, :].rearrange("p h d -> p (h d)"), ps[:, W_BANKS[i], :], OUT_SCALE).then_inc(su_ev, 1)

            def act_norm(phase):
                def f(g, j):
                    n = g + phase * G
                    act.wait_ge(shift_ready, count(n + 1))
                    if above_0(n - 1):
                        act.wait_ge(tr_done, count(n - 1))
                    nc.scalar.copy(act_pause[:, j:j + 1], shift[:, j, 0:1])
                    for t in range(GT - ACT_TILES[phase], GT):
                        last = nc.scalar.activation(xn[:, j, t * D:(t + 1) * D], xg(g, t, 1), ACT.Identity,
                                                    bias=shift[:, j, t:t + 1], scale=rstd[:, j, t:t + 1])
                    last.then_inc(xn_act_ready, 1)
                return f

            def xT_out(phase):
                def f(g, j):
                    act.wait_ge(tr_done, count(g + (phase * G + 1)))
                    if phase == LIN and (isinstance(g, Count) or g >= 2):
                        act.wait_ge(q_done, count(g - 1))
                        act.wait_ge(kv_done, count(g - 1))
                    else:
                        if above_0(g + (phase * G - 1)):
                            act.wait_ge(mm_done, count(g + (phase * G - 1)))
                    nc.scalar.copy(xT[:, j, :], ps[:, 0 if phase == LIN else j, :]).then_inc(xT_ready, 1)
                return f

            def tanh(phase, k):
                def f(g, j):
                    act.wait_ge(mm_done, count(g + (phase * G + 1)))
                    if above_0(g + (phase * G - 1)):
                        act.wait_ge(x_ready, count(g + (phase * G - 1)))
                    nc.scalar.activation(th[:, j, :], ps[:, BANK_OUT + j, :], ACT.Tanh).then_inc(th_ready, 1)
                return f

            def exp_k(g, j):
                act.wait_ge(kv_done, count(g + 1))
                if above_0(2 * g - 1):
                    act.wait_ge(phi_ready, count(2 * g - 1))
                nc.scalar.activation(ek[:], kv[:, :, 0:P], ACT.Exp, bias=-1.0).then_inc(ek_ready, 1)

            def values_lin(g, j):
                if above_0(g):
                    act.wait_ge(ctx_done, count(g))
                nc.scalar.copy(vones[:, :, 0:P], kv[:, :, P:2 * P]).then_inc(v0_ready, 1)

            def exp_q(g, j):
                act.wait_ge(q_done, count(g + 1))
                if above_0(2 * g):
                    act.wait_ge(phi_ready, count(2 * g))
                nc.scalar.activation(eq[:], ps[:, LIN_Q, :], ACT.Exp, bias=-1.0).then_inc(eq_ready, 1)

            def y0T_out(g, j):
                act.wait_ge(y0t_done, count(g + 1))
                act.wait_ge(mm_done, count(g + G))
                nc.scalar.copy(yT0[:], ps[:, LIN_C, :]).then_inc(yT0_ready, 1)

            phases(act, [[(2, xT_out(FFN1)), (3, act_norm(FFN1)), (1, tanh(FFN1, 0))],
                         [(3, act_norm(LIN)), (1, exp_k), (1, values_lin), (0, y0T_out), (1, exp_q), (2, xT_out(LIN))],
                         [(2, xT_out(FFN2)), (3, act_norm(FFN2)), (1, tanh(FFN2, 1))],
                         [(2, xT_out(SPEC1)), (3, act_norm(SPEC1))]],
                   early={0: small_out})

            def x_high(b, j):
                act.wait_ge(tr_done, count(b + (SOFT + 1)))
                if above_0(2 * PAIRS * (b - 1)):
                    act.wait_ge(s_done, count(2 * PAIRS * (b - 1)))
                nc.scalar.copy(x_hi[:, j, :], ps[:, BANK_X, 0:T]).then_inc(xhi_ready, 1)

            def u_high(n, j):
                act.wait_ge(u_done, count(n + 1))
                if above_0(2 * n - 2):
                    act.wait_ge(s_done, count(2 * n - 2))
                nc.scalar.copy(u_hi[:, j].rearrange("p h k -> p (h k)"), ps[:, BANK_U, :]).then_inc(uhi_ready, 1)

            def exp_tile(n, j, qt):
                act.wait_ge(max_ready, count(2 * n + (1 + qt)))
                if qt == 0:
                    if above_0(n - 1):
                        act.wait_ge(pt_done, count(n - 1))
                    if above_0(n - 1):
                        act.wait_ge(rinv_ready, count(n - 1))
                w = (qt + 1) * P
                for h in range(2):
                    at = 2 * h + qt
                    dst = pr[:, j, h, 0, :] if qt == 0 else pr[:, j, h, 1:3, :].rearrange("p b k -> p (b k)")
                    last = nc.scalar.activation(dst, ps[:, BANK_S + 2 * j + qt, h * w:(h + 1) * w], ACT.Exp,
                                                bias=neg_max[:, j, at:at + 1], scale=-1.0, accum_out=rsum[:, j, at:at + 1])
                last.then_inc(exp_ready, 1)

            def probs_T(n, j):
                act.wait_ge(pt_done, count(n + 1))
                if above_0(n - 1):
                    act.wait_ge(pv_done, count(n - 1))
                nc.scalar.copy(pT[:, j].rearrange("p h b q -> p (h b q)")[:, 512:768], ps[:, BANK_T + 1, 0:256]).then_inc(pTb_ready, 1)

            def values_out(b, j, c, bank=BANK_X):
                act.wait_ge(v_done, count(4 * b + (c + 1)))
                if c == 0:
                    if above_0(PAIRS * (b - 1)):
                        act.wait_ge(pv_done, count(PAIRS * (b - 1)))
                nc.scalar.copy(vv[:, j, c % 2, 512 * (c // 2):512 * (c // 2) + 512], ps[:, bank, :]).then_inc(v_ready, 1)

            def y_out(b, jb, p):
                act.wait_ge(pv_done, count(b * PAIRS + (p + 1)))
                if p == 0:
                    if above_0(b - 1):
                        act.wait_ge(w_done, count(b - 1))
                nc.scalar.copy(yT[:, jb, p, :], y_bank).then_inc(y_ready, 1)

            def z_xT_out(b):
                act.wait_ge(z_tr_done, count(b + 1))
                if above_0(b):
                    act.wait_ge(w_done, count(b + 1))
                nc.scalar.copy(z_xT[:], ps[:, BANK_X, 0:T]).then_inc(z_xT_ready, 1)

            g_high()
            x_high(0, 0)
            v_high()
            w_out()
            u_high(0, 0)
            for c in range(2):
                values_out(0, 0, c, FIRST_V_BANKS[c])
            u_high(1, 1)
            values_out(0, 0, 2, FIRST_V_BANKS[2])
            u_high(2, 0)
            exp_tile(0, 0, 0)
            exp_tile(0, 0, 1)
            values_out(0, 0, 3, FIRST_V_BANKS[3])

            def batch(b, jb, first=False, last=False):
                for p in range(PAIRS):
                    n, j = b * PAIRS + p, p % 2
                    if not (first and p == 0):
                        probs_T(n - 1, 1 - j)
                    if not (last and p >= PAIRS - 3):
                        u_high(n + 3, 1 - j)
                    if not (last and p >= PAIRS - 1):
                        exp_tile(n + 1, 1 - j, 0)
                    if p > 0:
                        y_out(b, jb, p - 1)
                    elif not first:
                        y_out(b - 1, 1 - jb, PAIRS - 1)
                    if not (last and p >= PAIRS - 1):
                        exp_tile(n + 1, 1 - j, 1)
                    if p == 0 and above_0(b - 1):
                        z_xT_out(b - 2)
                    if p == 2 and not last:
                        x_high(b + 1, 1 - jb)
                    if p >= V_TURN and not last:
                        values_out(b + 1, 1 - jb, p - V_TURN)

            batches(act, batch)
            probs_T(B * PAIRS - 1, 1)
            y_out(B - 1, 1, PAIRS - 1)
            z_xT_out(B - 2)
            z_xT_out(B - 1)

        @block.tensor
        def _(pe):
            mm, tr = nc.tensor.matmul, nc.tensor.transpose
            wu_kv = wu_s[:].rearrange("r (h s e) -> r s h e", s=2, e=E0)
            pe.wait_ge(pool_const, 3)
            pe.wait_ge(in_ffn, 16 * FFN_LOADS)
            tr(ps[:, 0, 0:D], w123_s[:, 0, :], ident[:])
            tr(ps[:, 0, D:2 * D], w123_s[:, 1, :], ident[:]).then_inc(su_pe, 1)
            pe.wait_ge(su_ev, 1)
            mm(ps[:, 2, 0:D], wt_s[:, 1, :], w123_s[:, 2, :], start=True, stop=True).then_inc(su_pe, 1)
            pe.wait_ge(su_ev, 2)
            mm(ps[:, 3, 0:D], wt_s[:, 0, :], w23[:], start=True, stop=True).then_inc(su_pe, 1)
            pe.wait_ge(su_ev, 3)

            def small_products():
                pe.wait_ge(in_small, 16 * SMALL_LOADS)
                tr(ps[0:R, 2, 0:D], wd_s[:], ident[:])
                cos, sin, nsin = (dft_s[:, k, :] for k in range(3))
                mm(ps[:, 3, 0:D], wre_s[:], cos, start=True, stop=False, skip_group_check=True)
                mm(ps[:, 3, 0:D], wim_s[:], sin, start=False, stop=True, skip_group_check=True)
                mm(ps[:, 3, D:2 * D], wim_s[:], cos, start=True, stop=False, skip_group_check=True)
                mm(ps[:, 3, D:2 * D], wre_s[:], nsin, start=False, stop=True, skip_group_check=True).then_inc(su_pe, 1)
                pe.wait_ge(su_ev, 4)
                for s in range(2):
                    mm(ps[:, 4, s * D:(s + 1) * D], wt_s[0:R, 2, :], wu_kv[:, s], start=True, stop=True)
                for s in range(2):
                    mm(ps[0:1, 7, s * D:(s + 1) * D], bd_s[:], wu_kv[:, s], start=True, stop=True)
                mm(ps[:, 2, D:2 * D], abT[:, 0, :], cos, start=True, stop=False, skip_group_check=True)
                mm(ps[:, 2, D:2 * D], abT[:, 1, :], sin, start=False, stop=True, skip_group_check=True).then_inc(su_pe, 1)

            def g_weights():
                pe.wait_ge(in_qk, 32)
                q_h = q_raw.rearrange("q (d h) -> q h d", h=H)
                k_h = k_raw.rearrange("q (d h) -> q h d", h=H)
                for h in range(H):
                    last = mm(ps[:, h // 4, (h % 4) * D:(h % 4 + 1) * D], k_h[:, h, :], q_h[:, h, :], start=True, stop=True)
                    if h % 4 == 3:
                        last.then_inc(su_pe, 1)

            def v_weights():
                pe.wait_ge(in_vw, 32)
                v_h = v_raw.rearrange("v (d h) -> v h d", h=H)
                for h in range(H):
                    last = tr(ps[:, V_BANKS[h // 8], (h % 8) * DV:(h % 8 + 1) * DV], v_h[:, h, :], ident[0:DV, 0:DV])
                    if h % 8 == 7:
                        last.then_inc(su_pe, 1)

            def out_weights():
                pe.wait_ge(w_heads_ready, 1)
                pe.wait_ge(su_lo, 1)
                for p in range(PAIRS):
                    last = tr(ps[:, W_BANKS[p // 4], (p % 4) * D:(p % 4 + 1) * D], w_heads[:, p * P:(p + 1) * P], ident[:])
                    if p % 4 == 3:
                        last.then_inc(su_pe, 1)

            def transpose(phase):
                def f(g, j):
                    n = g + phase * G
                    pe.wait_ge(xn_ready, count(g + (phase * G + 1)))
                    pe.wait_ge(xn_act_ready, count(n + 1))
                    if phase == LIN or isinstance(g, int) and g == 0:
                        if above_0(n):
                            pe.wait_ge(xT_ready, count(n))
                    elif above_0(n - 1):
                        pe.wait_ge(xT_ready, count(n - 1))
                    if phase == FFN2 and isinstance(g, int) and g == 1:
                        pe.wait_ge(phi_ready, 2 * G)
                    for t in range(GT):
                        last = tr(ps[:, 0 if phase == LIN else j, t * P:(t + 1) * P], xn[:, j, t * D:(t + 1) * D], ident[:])
                    last.then_inc(tr_done, 1)
                return f

            def bias_rows(at, n):
                return bias_bf[:, at:at + n].unsqueeze(1).to_broadcast([P, 512 // n, n])

            def product(phase, w, bias, freed, before):
                def f(g, j):
                    pe.wait_ge(xT_ready, count(g + (phase * G + 1)))
                    if phase == FFN1 and isinstance(g, int) and g == 0:
                        pe.wait_ge(bias_ready, 1)
                    if phase == FFN2 and isinstance(g, int) and g == 0:
                        pe.wait_ge(y0_ready, G)
                    if above_0(g + (before - 1)):
                        pe.wait_ge(freed, count(g + (before - 1)))
                    bank = ps[:, BANK_OUT + j, :]
                    mm(bank.rearrange("p (t d) -> p t d", d=D), ones_bf[:, 0:P], bias_rows(bias, D), start=True, stop=False,
                       skip_group_check=True)
                    for t in range(GT):
                        last = mm(bank[:, t * D:(t + 1) * D], xT[:, j, t * P:(t + 1) * P], w, start=False, stop=True,
                                  skip_group_check=True)
                    last.then_inc(mm_done, 1)
                return f

            def keys_values(g, j):
                pe.wait_ge(xT_ready, count(g + (G + 1)))
                if above_0(g):
                    pe.wait_ge(v0_ready, count(g))
                    pe.wait_ge(phi_ready, count(2 * g - 1))
                if isinstance(g, int) and g == 0:
                    pe.wait_ge(su_ev, 5)
                    pe.wait_ge(bias_ready, 2)
                for k in range(2):
                    bank = ps[:, LIN_KV + k, :]
                    mm(bank.rearrange("p (t d) -> p t d", d=2 * D), ones_bf[:, 0:P], bias_rows(KV_B, 2 * D), start=True, stop=False,
                       skip_group_check=True)
                    for t in range(2):
                        last = mm(bank[:, t * 2 * D:(t + 1) * 2 * D], xT[:, j, (2 * k + t) * P:(2 * k + t + 1) * P],
                                  wkv[:], start=False, stop=True, skip_group_check=True)
                last.then_inc(kv_done, 1)

            def queries(g, j):
                if above_0(2 * g):
                    pe.wait_ge(phi_ready, count(2 * g))
                mm(ps[:, LIN_Q, :], bias_bf[:, BQ:BQ + D], ones_bf[:], start=True, stop=False, skip_group_check=True)
                mm(ps[:, LIN_Q, :], wq_s[:], xT[:, j, :], start=False, stop=True, skip_group_check=True).then_inc(q_done, 1)

            def lin_context(g, j):
                pe.wait_ge(phi_ready, count(2 * g + 1))
                if above_0(g):
                    pe.wait_ge(yT0_ready, count(g))
                for b in range(GB):
                    for t in range(BT):
                        last = mm(ps[:, LIN_C, b * 2 * P:b * 2 * P + P + 1], phk[:, b * BT + t, :], vones[:, b * BT + t, :],
                                  start=(t == 0), stop=(t == BT - 1))
                last.then_inc(ctx_done, 1)

            def lin_outputs(g, j):
                pe.wait_ge(cbd_ready, count(g + 1))
                pe.wait_ge(phi_ready, count(2 * g + 2))
                if isinstance(g, int) and g == 0:
                    pe.wait_ge(th_ready, G)
                if above_0(g):
                    pe.wait_ge(y0_ready, count(g))
                for t in range(GT):
                    last = mm(num_den[:, t, 0:P + H0], phq[:, j, t * P:(t + 1) * P], cbd[:, t // BT, :],
                              start=True, stop=True, skip_group_check=True)
                last.then_inc(nd_done, 1)

            def y0_transpose(g, j):
                pe.wait_ge(y0_ready, count(g + 1))
                for t in range(GT):
                    last = tr(ps[:, LIN_C, t * P:(t + 1) * P], y0[:, t, :], ident[:])
                last.then_inc(y0t_done, 1)

            def lin_project_out(g, j):
                pe.wait_ge(yT0_ready, count(g + 1))
                pe.wait_ge(x_ready, count(g + G))
                mm(ps[:, LIN_O, :].rearrange("p (t d) -> p t d", d=D), ones_bf[:, 0:P], bias_rows(BO_B, D), start=True, stop=False,
                   skip_group_check=True)
                for t in range(GT):
                    last = mm(ps[:, LIN_O, t * D:(t + 1) * D], yT0[:, t * P:(t + 1) * P], wo_s[:], start=False, stop=True,
                              skip_group_check=True)
                last.then_inc(mm_done, 1)

            phases(pe, [[(2, transpose(FFN1)), (1, product(FFN1, wc[:], FFN_B, th_ready, 0))],
                        [(0, lin_outputs), (1, keys_values), (0, y0_transpose), (1, queries), (2, transpose(LIN)),
                         (1, lin_context), (0, lin_project_out)],
                        [(2, transpose(FFN2)), (1, product(FFN2, wc[:], FFN_B, th_ready, G))],
                        [(2, transpose(SPEC1)), (1, product(SPEC1, circ[:], FFT_B, x_ready, 3 * G))]],
                   early={0: small_products})

            def x_transpose(b, j):
                pe.wait_ge(xn_ready, count(b + (SOFT + 1)))
                for t in range(BT):
                    last = tr(ps[:, BANK_X, t * P:(t + 1) * P], xn[:, j, t * D:(t + 1) * D], ident[:])
                last.then_inc(tr_done, 1)

            def u_product(n, h2, jb, j):
                for k in range(2):
                    h = 2 * h2 + k
                    o = ps[:, BANK_U, k * T:(k + 1) * T]
                    mm(o, g_hi[:, h, :], x_hi[:, jb, :], start=True, stop=False, skip_group_check=True)
                    mm(o, g_hi[:, h, :], x_lo[:, jb, :], start=False, stop=False, skip_group_check=True)
                    last = mm(o, g_lo[:, h, :], x_hi[:, jb, :], start=False, stop=True, skip_group_check=True)
                last.then_inc(u_done, 1)

            def scores(n, jb, j):
                pe.wait_ge(ulo_ready, count(n + 1))
                if above_0(2 * n - 3):
                    pe.wait_ge(exp_ready, count(2 * n - 3))
                o = ps[:, BANK_S + 2 * j, 0:2 * P].rearrange("p (h k) -> p h k", h=2)
                uh, ul = (a[:, j, :, 0:P] for a in (u_hi, u_lo))
                xh, xl = x_hi[:, jb, 0:P], x_lo[:, jb, 0:P]
                mm(o, xh, uh, start=True, stop=False, skip_group_check=True)
                mm(o, xh, ul, start=False, stop=False, skip_group_check=True)
                mm(o, xl, uh, start=False, stop=True, skip_group_check=True).then_inc(s_done, 1)
                if above_0(2 * n - 2):
                    pe.wait_ge(exp_ready, count(2 * n - 2))
                o = ps[:, BANK_S + 2 * j + 1, :].rearrange("p (h k) -> p h k", h=2)
                uh, ul = u_hi[:, j], u_lo[:, j]
                xh, xl = x_hi[:, jb, P:2 * P], x_lo[:, jb, P:2 * P]
                mm(o, xh, uh, start=True, stop=False, skip_group_check=True)
                mm(o, xh, ul, start=False, stop=False, skip_group_check=True)
                mm(o, xl, uh, start=False, stop=True, skip_group_check=True).then_inc(s_done, 1)

            def probs_transpose(n, j):
                pe.wait_ge(pn_ready, count(n + 1))
                if above_0(n):
                    pe.wait_ge(pTa_ready, count(n))
                for k in range(6):
                    if k == 4 and above_0(n):
                        pe.wait_ge(pTb_ready, count(n))
                        pe.wait_ge(y_ready, count(n))
                    last = tr(ps[:, BANK_T + k // 4, (k % 4) * P:(k % 4 + 1) * P], pr[:, j, k // 3, k % 3, :], ident[:])
                last.then_inc(pt_done, 1)

            def values(b, j, c, bank=BANK_X):
                at = slice(512 * (c // 2), 512 * (c // 2) + 512)
                tok = slice((c % 2) * P, (c % 2 + 1) * P)
                mm(ps[:, bank, :], x_hi[:, j, tok], v_hi[:, at], start=True, stop=False, skip_group_check=True)
                mm(ps[:, bank, :], x_hi[:, j, tok], v_lo[:, at], start=False, stop=False, skip_group_check=True)
                mm(ps[:, bank, :], x_lo[:, j, tok], v_hi[:, at], start=False, stop=True, skip_group_check=True).then_inc(v_done, 1)

            def products(n, p, jb, j):
                pe.wait_ge(pTa_ready, count(n + 1))
                pe.wait_ge(pTb_ready, count(n + 1))
                for kt in range(BT):
                    for k in range(2):
                        h = 2 * p + k
                        last = mm(y_bank[k * DV:(k + 1) * DV, kt * P:T], vv[:, jb, kt, h * DV:(h + 1) * DV],
                                  pT[:, j, k, 0:2, :] if kt == 0 else pT[:, j, k, 2, :], start=(kt == 0), stop=(kt == 1),
                                  skip_group_check=True)
                last.then_inc(pv_done, 1)

            def project_out(b, j):
                pe.wait_ge(y_ready, count(PAIRS * (b + 1)))
                for t in range(BT):
                    for p in range(PAIRS):
                        last = mm(ps[:, BANK_X, t * D:(t + 1) * D], yT[:, j, p, t * P:(t + 1) * P], wz[:, p, :],
                                  start=(p == 0), stop=(p == PAIRS - 1), skip_group_check=True)
                if not above_0(b):
                    last.then_inc(w_done, 1)

            def spectral_transpose(b):
                pe.wait_ge(z_xn_ready, count(b + 1))
                for t in range(BT):
                    last = tr(ps[:, BANK_X, t * P:(t + 1) * P], z_xn[:, t * D:(t + 1) * D], ident[:])
                last.then_inc(z_tr_done, 1)

            def spectral_product(b):
                o = ps[:, BANK_X, BT * D:]
                mm(o.rearrange("p (t d) -> p t d", d=D), ones_bf[:, 0:P],
                   bias_bf[:, FFT_B:FFT_B + D].unsqueeze(1).to_broadcast([P, BT, D]), start=True, stop=False, skip_group_check=True)
                for t in range(BT):
                    last = mm(o[:, t * D:(t + 1) * D], z_xT[:, t * P:(t + 1) * P], circ[:], start=False, stop=True,
                              skip_group_check=True)
                last.then_inc(w_done, 1)

            g_weights()
            pe.wait_ge(x_ready, 4 * G)
            x_transpose(0, 0)
            v_weights()
            out_weights()
            pe.wait_ge(su_lo, 4)
            pe.wait_ge(xlo_ready, 1)
            pe.wait_ge(su_ev, 6)
            u_product(0, 0, 0, 0)
            pe.wait_ge(su_lo, 6)
            values(0, 0, 0)
            pe.wait_ge(su_ev, 7)
            values(0, 0, 1, FIRST_V_BANKS[1])
            pe.wait_ge(ulo_ready, 1)
            u_product(1, 1, 0, 1)
            scores(0, 0, 0)
            values(0, 0, 2, FIRST_V_BANKS[2])
            pe.wait_ge(ulo_ready, 2)
            u_product(2, 2, 0, 0)
            scores(1, 0, 1)
            pe.wait_ge(v_ready, 1)
            values(0, 0, 3)
            pe.wait_ge(v_ready, 3)

            def batch(b, jb, first=False, last=False):
                for p in range(PAIRS):
                    n, j = b * PAIRS + p, p % 2
                    if not (last and p >= PAIRS - 3):
                        pe.wait_ge(ulo_ready, count(n + 3))
                        u_product(n + 3, (p + 3) % PAIRS, jb if p + 3 < PAIRS else 1 - jb, 1 - j)
                    if not (last and p >= PAIRS - 2):
                        scores(n + 2, jb if p + 2 < PAIRS else 1 - jb, j)
                    if p > 0:
                        products(n - 1, p - 1, jb, 1 - j)
                    elif not first:
                        products(n - 1, PAIRS - 1, 1 - jb, 1 - j)
                    if p == 0 and above_0(b - 1):
                        pe.wait_ge(v_ready, count(4 * (b + 1)))
                        spectral_transpose(b - 2)
                    if p == 1 and not first:
                        if above_0(b - 1):
                            pe.wait_ge(z_xT_ready, count(b - 1))
                        else:
                            pe.wait_ge(v_ready, 8)
                        project_out(b - 1, 1 - jb)
                        if above_0(b - 1):
                            spectral_product(b - 2)
                    if p == 2 and not last:
                        if first:
                            pe.wait_ge(v_ready, 4)
                        else:
                            pe.wait_ge(x_ready, count(b + SOFT))
                        if above_0(b - 1):
                            pe.wait_ge(out_ready, count(b - 1))
                        x_transpose(b + 1, 1 - jb)
                    if p == V_TURN and not last:
                        pe.wait_ge(xlo_ready, count(b + 2))
                    if p > V_TURN and not last:
                        pe.wait_ge(v_ready, count(4 * (b + 1) + (p - V_TURN)))
                    if p >= V_TURN and not last:
                        values(b + 1, 1 - jb, p - V_TURN)
                    probs_transpose(n, j)

            batches(pe, batch)
            products(B * PAIRS - 1, PAIRS - 1, 1, 1)
            pe.wait_ge(out_ready, B - 2)
            spectral_transpose(B - 2)
            pe.wait_ge(z_xT_ready, B - 1)
            project_out(B - 1, 1)
            spectral_product(B - 2)
            pe.wait_ge(out_ready, B - 1)
            spectral_transpose(B - 1)
            pe.wait_ge(z_xT_ready, B)
            spectral_product(B - 1)


_INS = ["L0_attn_x", "L0_attn_Wq", "L0_attn_bq", "L0_attn_Wd", "L0_attn_bd", "L0_attn_Wu", "L0_attn_bu",
        "L0_attn_Wo", "L0_attn_bo", "L0_ffn_weight", "L0_ffn_aux_weight1", "L0_ffn_aux_weight2", "L0_ffn_bias",
        "L1_attn_Q", "L1_attn_K", "L1_attn_V", "L1_attn_W", "L1_ffn_w_freq_real", "L1_ffn_w_freq_imag", "L1_ffn_bias"]


def dft_tables():
    a = 2 * np.pi / D * (np.arange(D)[:, None] * np.arange(D)[None, :] % D)
    return np.concatenate([np.cos(a), np.sin(a), -np.sin(a)], axis=1).astype(np.float32)


def kernel(**inputs):
    import concourse.bacc as bacc
    from concourse.bass_utils import run_bass_kernel_spmd

    nc = bacc.Bacc("TRN2", target_bir_lowering=False, num_devices=1)
    arrays, args = {}, []
    for name in _INS:
        a = np.ascontiguousarray(inputs[name])
        arrays[name] = a
        args.append(nc.dram_tensor(name, a.shape, mybir.dt.from_np(a.dtype), kind="ExternalInput").ap())
    arrays["dft"] = dft_tables()
    args.append(nc.dram_tensor("dft", (D, 3 * D), F32, kind="ExternalInput").ap())
    args.append(nc.dram_tensor("out", (B, T, D), F32, kind="ExternalOutput").ap())
    build(nc, *args)
    r = run_bass_kernel_spmd(nc, [arrays], core_ids=[0])
    return r.results[0]["out"]
```
